# Optimizing a Trainium2 kernel written in Bass

```python
import numpy as np
import jax
import jax.numpy as jnp

def _softmax(x, axis=-1):
    return jax.nn.softmax(x, axis=axis)

def _gelu(x):
    return jax.nn.gelu(x, approximate=True)

def _silu(x):
    return jax.nn.silu(x)

def _sigmoid(x):
    return jax.nn.sigmoid(x)

def _layernorm(x, axis=-1, eps=1e-05):
    m = jnp.mean(x, axis=axis, keepdims=True)
    v = jnp.var(x, axis=axis, keepdims=True)
    return (x - m) / jnp.sqrt(v + eps)

def _scatter_add(tgt, idx, src, axis=0):
    return tgt.at[idx].add(src)

def _segment_sum(src, seg, n):
    return jax.ops.segment_sum(src, seg, n)
kernel_name = 'mk_gnn_resnorm_d2_gnn_r8_b28215'

def setup_inputs(seed: int=0):
    np.random.seed(seed)
    _w = jnp.asarray

    def _rec_inputs():
        import jax
        import jax.numpy as jnp
        _gk = jax.random.key(seed)
        x = -0.0001006 + 1 * jax.random.normal(jax.random.fold_in(_gk, 1), (6250, 96), jnp.float32)
        _s = jax.random.randint(jax.random.fold_in(_gk, 2), (100000,), 0, 6250, jnp.int32)
        _d = jax.random.randint(jax.random.fold_in(_gk, 3), (100000,), 0, 6250, jnp.int32)
        _loop = jnp.arange(6250, dtype=jnp.int32)
        src = jnp.concatenate([_s, _d, _loop])
        dst = jnp.concatenate([_d, _s, _loop])
        _o = jnp.argsort(dst, stable=True)
        src = src[_o]
        dst = dst[_o]
        edge_attr_32 = 0.000196303 + 1.00016 * jax.random.normal(jax.random.fold_in(_gk, 12), (206250, 32), jnp.float32)
        return (x, src, dst, edge_attr_32)
    x, src, dst, edge_attr_32 = _rec_inputs()

    def _L0_gnn_setup():
        import jax, jax.numpy as jnp
        import numpy as np
        N_NODES = 6250
        N_EDGES = 100000
        D_FEAT = 96
        L = 0.5
        key = jax.random.key(seed)
        k1, k2, k3 = jax.random.split(key, 3)
        h = jax.random.normal(k1, (N_NODES, D_FEAT), dtype=jnp.float32)
        src = jax.random.randint(k2, (N_EDGES,), 0, N_NODES, dtype=jnp.int64)
        dst = jax.random.randint(k3, (N_EDGES,), 0, N_NODES, dtype=jnp.int64)
        return {'h': h, 'src': src, 'dst': dst}
    _L0_gnn_all = _L0_gnn_setup()
    _L0_gnn_in = {k: v for k, v in _L0_gnn_all.items() if k in ()}
    del _L0_gnn_all

    def _L1_gnn_setup():
        import jax, jax.numpy as jnp
        import numpy as np
        N, E = (6250, 100000)
        ND, ED = (96, 32)

        def _gelu(x):
            return jax.nn.gelu(x, approximate=False)
        key = jax.random.key(seed)
        ks = jax.random.split(key, 16)
        s = lambda fan_in: 1.0 / np.sqrt(fan_in)
        inp = {'x': jax.random.normal(ks[0], (N, ND), jnp.float32), 'edge_index': jax.random.randint(ks[1], (2, E), 0, N, jnp.int32), 'edge_attr': jax.random.normal(ks[2], (E, ED), jnp.float32), 'mW1': jax.random.uniform(ks[3], (ND + ED, ND), jnp.float32, -s(ND + ED), s(ND + ED)), 'mb1': jnp.zeros((ND,), jnp.float32), 'mW2': jax.random.uniform(ks[4], (ND, ND), jnp.float32, -s(ND), s(ND)), 'mb2': jnp.zeros((ND,), jnp.float32), 'gW1': jax.random.uniform(ks[5], (ND + ED, ND), jnp.float32, -s(ND + ED), s(ND + ED)), 'gb1': jnp.zeros((ND,), jnp.float32), 'gW2': jax.random.uniform(ks[6], (ND, 1), jnp.float32, -s(ND), s(ND)), 'gb2': jnp.zeros((1,), jnp.float32), 'uW1': jax.random.uniform(ks[7], (2 * ND, ND), jnp.float32, -s(2 * ND), s(2 * ND)), 'ub1': jnp.zeros((ND,), jnp.float32), 'uW2': jax.random.uniform(ks[8], (ND, ND), jnp.float32, -s(ND), s(ND)), 'ub2': jnp.zeros((ND,), jnp.float32), 'ln_g': jnp.ones((ND,), jnp.float32), 'ln_b': jnp.zeros((ND,), jnp.float32)}
        return inp
    _L1_gnn_all = _L1_gnn_setup()
    _L1_gnn_in = {k: v for k, v in _L1_gnn_all.items() if k in ('mW1', 'mb1', 'mW2', 'mb2', 'gW1', 'gb1', 'gW2', 'gb2', 'uW1', 'ub1', 'uW2', 'ub2', 'ln_g', 'ln_b')}
    del _L1_gnn_all
    return {'x': x, 'src': src, 'dst': dst, 'edge_attr_32': edge_attr_32, 'L1_gnn_mW1': _L1_gnn_in['mW1'], 'L1_gnn_mb1': _L1_gnn_in['mb1'], 'L1_gnn_mW2': _L1_gnn_in['mW2'], 'L1_gnn_mb2': _L1_gnn_in['mb2'], 'L1_gnn_gW1': _L1_gnn_in['gW1'], 'L1_gnn_gb1': _L1_gnn_in['gb1'], 'L1_gnn_gW2': _L1_gnn_in['gW2'], 'L1_gnn_gb2': _L1_gnn_in['gb2'], 'L1_gnn_uW1': _L1_gnn_in['uW1'], 'L1_gnn_ub1': _L1_gnn_in['ub1'], 'L1_gnn_uW2': _L1_gnn_in['uW2'], 'L1_gnn_ub2': _L1_gnn_in['ub2'], 'L1_gnn_ln_g': _L1_gnn_in['ln_g'], 'L1_gnn_ln_b': _L1_gnn_in['ln_b']}

def reference(x, src, dst, edge_attr_32, L1_gnn_mW1, L1_gnn_mb1, L1_gnn_mW2, L1_gnn_mb2, L1_gnn_gW1, L1_gnn_gb1, L1_gnn_gW2, L1_gnn_gb2, L1_gnn_uW1, L1_gnn_ub1, L1_gnn_uW2, L1_gnn_ub2, L1_gnn_ln_g, L1_gnn_ln_b):
    import jax
    import jax.numpy as jnp

    def _L0_gnn_ref(h, src, dst):
        import jax, jax.numpy as jnp
        import numpy as np
        N_NODES = 6250
        N_EDGES = 100000
        D_FEAT = 96
        L = 0.5
        N = h.shape[0]
        deg = jax.ops.segment_sum(jnp.ones_like(dst, dtype=h.dtype), dst, num_segments=N)
        inv_deg = (1.0 / jnp.maximum(deg, 1.0))[:, None]

        def mean_agg(x):
            msg_sum = jax.ops.segment_sum(x[src], dst, num_segments=N)
            return msg_sum * inv_deg
        neigh1 = mean_agg(h)
        neigh2 = mean_agg(neigh1)
        return L * neigh1 + (1.0 - L) * neigh2

    def _L1_gnn_ref(x, edge_index, edge_attr, mW1, mb1, mW2, mb2, gW1, gb1, gW2, gb2, uW1, ub1, uW2, ub2, ln_g, ln_b):
        import jax, jax.numpy as jnp
        import numpy as np
        N, E = (6250, 100000)
        ND, ED = (96, 32)

        def _gelu(x):
            return jax.nn.gelu(x, approximate=False)
        src, dst = (edge_index[0], edge_index[1])
        edge_input = jnp.concatenate([x[src], edge_attr], axis=-1)
        messages = _gelu(edge_input @ mW1 + mb1) @ mW2 + mb2
        gates = jax.nn.sigmoid(_gelu(edge_input @ gW1 + gb1) @ gW2 + gb2)
        aggregated = jax.ops.segment_sum(messages * gates, dst, num_segments=x.shape[0])
        combined = jnp.concatenate([x, aggregated], axis=-1)
        update = _gelu(combined @ uW1 + ub1) @ uW2 + ub2
        h = x + update
        mu = jnp.mean(h, axis=-1, keepdims=True)
        var = jnp.mean(jnp.square(h - mu), axis=-1, keepdims=True)
        return (h - mu) * jax.lax.rsqrt(var + 1e-05) * ln_g + ln_b
    edge_index = jnp.stack([src, dst])
    x = _layernorm(x + _L0_gnn_ref(x, src, dst), axis=-1)
    x = _layernorm(x + _L1_gnn_ref(x, edge_index, edge_attr_32, L1_gnn_mW1, L1_gnn_mb1, L1_gnn_mW2, L1_gnn_mb2, L1_gnn_gW1, L1_gnn_gb1, L1_gnn_gW2, L1_gnn_gb2, L1_gnn_uW1, L1_gnn_ub1, L1_gnn_uW2, L1_gnn_ub2, L1_gnn_ln_g, L1_gnn_ln_b), axis=-1)
    return x

_drawn_inputs = setup_inputs


def setup_inputs(seed=0):
    import zlib

    import numpy as np

    out = dict(_drawn_inputs(seed))
    spreads = {'L1_gnn_mb1': (0.0, 0.281),
     'L1_gnn_mb2': (0.0, 0.1),
     'L1_gnn_gb1': (0.0, 2.0),
     'L1_gnn_ub1': (0.0, 0.424),
     'L1_gnn_ub2': (0.0, 0.1),
     'L1_gnn_ln_g': (1.0, 0.2),
     'L1_gnn_ln_b': (0.0, 0.1)}
    factors = {'L1_gnn_gW1': 8.0, 'L1_gnn_gW2': 8.0}
    for name, (base, spread) in spreads.items():
        noise = np.random.default_rng([zlib.crc32(name.encode()), seed]).standard_normal(out[name].shape)
        drawn = base * np.exp(spread * noise) if base else spread * noise
        out[name] = jnp.asarray(drawn.astype(out[name].dtype))
    for name, factor in factors.items():
        out[name] = (out[name] * factor).astype(out[name].dtype)
    return out
```

```python
from contextlib import ExitStack

import concourse.bass as bass
from concourse import mybir

ALU = mybir.AluOpType
ACT = mybir.ActivationFunctionType
F32 = mybir.dt.float32
I32 = mybir.dt.int32
U32 = mybir.dt.uint32
AX_X = mybir.AxisListType.X

P = 128
N, E, D, DE = 6250, 206250, 96, 32
NT = -(-N // P)
NP = NT * P
GT = 8
GE = GT * P
NG = -(-E // GE)
RING = 4
ROUNDS = NG // RING
W = 64
NW = -(-(N + 1) // W)
AW = NP + W
DA = D + 1
D2 = 2 * D
C = 7
NC = NT // C
CN = C * P
HALF = GT // 2
EPS = 1e-5

assert NC * C == NT and (NG * GE - E) < GE and NW * W <= AW


def bass_gnn(nc, x, src, dst, ea, w_node, w_edge, w_msg2, w_gate2, b_gate2, w_upd1x, w_upd1a, b_upd1,
             w_upd2, ln_gb, out):
    neigh_table = nc.dram_tensor("neigh_table", [NP, D], F32, kind="Internal").ap()
    hidden_table = nc.dram_tensor("hidden_table", [NP, D2], F32, kind="Internal").ap()
    x_table = x.rearrange("p (t f) -> (p t) f", f=D)

    with ExitStack() as ctx:
        def sb(name, shape, dt=F32):
            return ctx.enter_context(nc.sbuf_tensor(name, shape, dt))

        def sem(name):
            return ctx.enter_context(nc.semaphore(name))

        ident = sb("ident", [P, P])
        iota_i = sb("iota_i", [P, W], I32)
        iota = sb("iota", [P, W])
        ones = sb("ones", [P, P])
        w_node_sb = sb("w_node_sb", [DA, D2])
        w_edge_sb = sb("w_edge_sb", [P, HALF, D2])
        w_msg2_sb = sb("w_msg2_sb", [DA, D])
        w_gate2_sb = sb("w_gate2_sb", [P, D])
        b_gate2_sb = sb("b_gate2_sb", [P, 1])
        half_b_gate2 = sb("half_b_gate2", [P, 1])
        w_upd1x_sb = sb("w_upd1x_sb", [D, D])
        w_upd1a_sb = sb("w_upd1a_sb", [D, D])
        b_upd1_sb = sb("b_upd1_sb", [D, 1])
        w_upd2_sb = sb("w_upd2_sb", [DA, D])
        ln_gb_sb = sb("ln_gb_sb", [P, 2 * D])

        local = sb("local", [P, NG, GT])
        ext = sb("ext", [P, 2, NG])
        ext_red = sb("ext_red", [P, 4])
        ext_diag = sb("ext_diag", [P, 4, P])
        spread = sb("spread", [P, NG])
        wide = sb("wide", [P, NG])
        first = sb("first", [P, NG])
        n_win = sb("n_win", [P, NG])
        first_i = sb("first_i", [1, NG], I32)
        n_win_i = sb("n_win_i", [1, NG], I32)

        idx = sb("idx", [P, RING, GT], I32)
        rows = sb("rows", [P, RING, GT, DA])
        hid = sb("hid", [P, RING, GT, D2 + 1])
        ea_sb = sb("ea_sb", [P, RING, 2 * P])
        here = sb("here", [P, GT])
        hot = sb("hot", [P, GT, W])
        prod = sb("prod", [P, GT, D])
        gate_dot = sb("gate_dot", [P, GT])
        gate_tanh = sb("gate_tanh", [P, GT])
        gate = sb("gate", [P, GT])
        acc_a = sb("acc_a", [DA, AW])
        acc_b = sb("acc_b", [DA, AW])

        x_nm = sb("x_nm", [P, NT, D])
        neigh_nm = sb("neigh_nm", [P, NT, D])
        dst_i = neigh_nm[:, :, :].rearrange("p t f -> p (t f)")[:, 0:NG * GT].bitcast(I32)
        inv_deg = sb("inv_deg", [P, NT])
        xT = sb("xT", [D, NC, CN])
        stage = sb("stage", [DA, C, P])
        stage_x = sb("stage_x", [DA, C, P])
        aggT = sb("aggT", [D, CN])
        updT = sb("updT", [DA, CN])
        t0 = sb("t0", [P, C, D])
        t1 = sb("t1", [P, C, D])
        t2 = sb("t2", [P, C, D])
        col = sb("col", [P, 4, C])
        hid_nm = sb("hid_nm", [P, C, D2])
        out_nm = neigh_nm

        psum = ctx.enter_context(nc.psum_tensor("psum", [P, 8, 512], F32))
        win_ps = psum[0:DA, 0, 0:W]
        pre_ps = [psum[:, 1 + 2 * h:3 + 2 * h, :].rearrange("p b (t n) -> p (b t) n", t=2)[:, :, 0:D2]
                  for h in range(2)]
        slots = psum[:, :, :].rearrange("p b (s n) -> p (b s) n", n=P)
        turned = slots[:, 0:C, :]
        turned_x = slots[:, 8:8 + C, :]
        hid_ps = psum[:, 4:8, :].rearrange("p b (t n) -> p (b t) n", t=2)[:, 0:C, 0:D2]

        s_weights = sem("s_weights")
        s_dst = sem("s_dst")
        s_x = sem("s_x")
        s_pool_const = sem("s_pool_const")
        s_pro = sem("s_pro")
        s_ext_turned = sem("s_ext_turned")
        s_ext_spread = sem("s_ext_spread")
        s_meta = sem("s_meta")
        s_ones = sem("s_ones")
        s_half_bias = sem("s_half_bias")

        class EdgePass:
            def __init__(self, name):
                self.idx_loaded = [sem(f"{name}_idx_loaded{k}") for k in range(RING)]
                self.gathered = [sem(f"{name}_gathered{k}") for k in range(RING)]
                self.row_free = [sem(f"{name}_row_free{k}") for k in range(RING)]
                self.here_set = sem(f"{name}_here_set")
                self.hot_set = sem(f"{name}_hot_set")
                self.here_moved = sem(f"{name}_here_moved")
                self.window_summed = sem(f"{name}_window_summed")
                self.window_added = sem(f"{name}_window_added")
                self.done = sem(f"{name}_done")

        pass1, pass2, pass3 = EdgePass("p1"), EdgePass("p2"), EdgePass("p3")
        ea_loaded = [sem(f"ea_loaded{k}") for k in range(RING)]
        pre_summed = sem("pre_summed")
        pre_added = sem("pre_added")
        hidden_done = sem("hidden_done")
        gate_prod = sem("gate_prod")
        gate_dotted = sem("gate_dotted")
        gate_tanhed = sem("gate_tanhed")
        gate_set = sem("gate_set")

        class NodePhase:
            def __init__(self, name):
                self.staged = sem(f"{name}_staged")
                self.turned = sem(f"{name}_turned")
                self.step = sem(f"{name}_step")
                self.var = sem(f"{name}_var")
                self.std = sem(f"{name}_std")
                self.normed = sem(f"{name}_normed")
                self.x_turned = sem(f"{name}_x_turned")
                self.x_staged = sem(f"{name}_x_staged")
                self.product = sem(f"{name}_product")
                self.copied = sem(f"{name}_copied")
                self.hidden = sem(f"{name}_hidden")
                self.stored = sem(f"{name}_stored")

        node1, node2, node3 = NodePhase("n1"), NodePhase("n2"), NodePhase("n3")

        block = ctx.enter_context(nc.Block())

        def steps(eng, sem_, base):
            n = [0]

            def step(ins):
                n[0] += 1
                ins.then_inc(sem_, 1)
                eng.wait_ge(sem_, base + n[0])
            return step, n

        def over_groups(eng, body, last=NG):
            with eng.Fori(0, last // RING) as i:
                for k in range(RING):
                    body(i * RING + k, k, i)
            for g in range(last // RING * RING, last):
                body(g, g % RING, g // RING)

        @block.sync
        def _(sp):
            def load_idx(ps, g, k):
                sp.dma_start(idx[:, k, :], src[bass.ds(g, 1), :, :].rearrange("g p t -> (g p) t")).then_inc(
                    ps.idx_loaded[k], 16)

            def load_ea(g, k):
                sp.dma_start(ea_sb[:, k, :], ea[bass.ds(g, 1), :, :].rearrange("g p n -> (g p) n")).then_inc(
                    ea_loaded[k], 16)

            for k in range(RING):
                load_idx(pass1, k, k)
            sp.dma_start(dst_i, dst).then_inc(s_dst, 16)
            for to, of in ((w_node_sb[:, :], w_node), (w_edge_sb[:, :, :].rearrange("p t n -> p (t n)"), w_edge), (w_msg2_sb[:, :], w_msg2), (w_gate2_sb[:, :], w_gate2),
                           (b_gate2_sb[:, :], b_gate2), (w_upd1x_sb[:, :], w_upd1x), (w_upd1a_sb[:, :], w_upd1a),
                           (b_upd1_sb[:, :], b_upd1), (w_upd2_sb[:, :], w_upd2), (ln_gb_sb[:, :], ln_gb)):
                sp.dma_start(to, of).then_inc(s_weights, 16)
            sp.dma_start(x_nm[:, :, :].rearrange("p t f -> p (t f)"), x).then_inc(s_x, 16)

            def feed(ps):
                def refill(g, k, i):
                    sp.wait_ge(ps.gathered[k], 16 * GT * (i + 1))
                    load_idx(ps, g + RING, k)
                over_groups(sp, refill, NG - RING)

            def store_table(node, table, of, f):
                view = table.rearrange("(p t) f -> p (t f)", p=P)
                with sp.Fori(0, NC) as c:
                    sp.wait_ge(node.copied, c + 2)
                    sp.dma_start(view[:, bass.ds(c * (C * f), C * f)], of(c)).then_inc(node.stored, 16)

            feed(pass1)
            for k in range(RING):
                sp.wait_ge(pass1.gathered[k], 16 * GT * len(range(k, NG, RING)))
                load_idx(pass2, k, k)
            flat = neigh_nm[:, :, :].rearrange("p t f -> p (t f)")
            store_table(node1, neigh_table, lambda c: flat[:, bass.ds(c * (C * D), C * D)], D)
            feed(pass2)
            for k in range(RING):
                sp.wait_ge(pass2.gathered[k], 16 * GT * len(range(k, NG, RING)))
                load_idx(pass3, k, k)
                load_ea(k, k)
            with sp.Fori(0, NC) as c:
                sp.wait_ge(node2.copied, c + 2)
                sp.dma_start(hidden_table.rearrange("(p t) f -> p (t f)", p=P)[:, bass.ds(c * (C * D2), C * D2)],
                             hid_nm[:, :, :].rearrange("p t f -> p (t f)")).then_inc(node2.stored, 16)

            def refill3(g, k, i):
                sp.wait_ge(pass3.gathered[k], 16 * GT * (i + 1))
                load_idx(pass3, g + RING, k)
                sp.wait_ge(pre_summed, 2 * g + 2)
                load_ea(g + RING, k)
            over_groups(sp, refill3, NG - RING)

            with sp.Fori(0, NC) as c:
                sp.wait_ge(node3.normed, c + 1)
                sp.dma_start(out[:, bass.ds(c * (C * D), C * D)],
                             out_nm[:, :, :].rearrange("p t f -> p (t f)")[:, bass.ds(c * (C * D), C * D)]).then_inc(
                    node3.stored, 16)
            sp.wait_ge(node3.stored, 16 * NC)

        @block.gpsimd
        def _(pool):
            nc.gpsimd.memset(ident[:], 0.0).then_inc(s_pool_const, 1)
            nc.gpsimd.iota(iota_i[:], pattern=[[1, W]], base=0, channel_multiplier=0).then_inc(s_pool_const, 1)
            pool.wait_ge(s_pool_const, 2)
            nc.gpsimd.affine_select(out=ident[:], in_=ident[:], compare_op=ALU.not_equal, fill=1.0, base=0,
                                    pattern=[[-1, P]], channel_multiplier=1).then_inc(s_pool_const, 1)

            def gather_all(ps, table, buf, width):
                def gather(g, k, i):
                    pool.wait_ge(ps.idx_loaded[k], 16 * (i + 1))
                    pool.wait_ge(ps.row_free[k], i + 1)
                    pool.nop(nofuse=True)
                    for t in range(GT):
                        pool.indirect_dma_start(
                            buf[:, k, t, 0:width], None, table,
                            bass.IndirectOffsetOnAxis(ap=idx[:, k, t:t + 1].bitcast(U32), axis=0),
                        ).then_inc(ps.gathered[k], 16)
                over_groups(pool, gather)

            gather_all(pass1, x_table, rows, D)
            pool.wait_ge(node1.stored, 16 * NC)
            gather_all(pass2, neigh_table, rows, D)
            pool.wait_ge(node2.stored, 16 * (NC + 1))
            gather_all(pass3, hidden_table, hid, D2)

        @block.tensor
        def _(pe):
            summed = pe.alloc_register("pe_windows")

            def sum_windows(ps, g, k, i, rhs_rows):
                n = pe.value_load(n_win_i[0:1, bass.ds(g, 1)], min_val=1, max_val=NW)
                with pe.Fori(0, n):
                    before = pe.snap(summed, min_val=0, max_val=NG * NW)
                    pe.wait_ge(ps.gathered[k], 16 * GT * (i + 1))
                    if ps is pass3:
                        pe.wait_ge(hidden_done, 2 * g + 2)
                    pe.wait_ge(ps.hot_set, before + 1)
                    pe.wait_ge(ps.window_added, before + 1)
                    for t in range(GT):
                        mm = nc.tensor.matmul(win_ps, rhs_rows(k, t), hot[:, t, :], start=(t == 0),
                                              stop=(t == GT - 1))
                    mm.then_inc(ps.window_summed, 1)
                    pe.reg_add(summed, summed, 1)

            pe.wait_ge(s_pool_const, 3)
            pe.wait_ge(s_pro, 2)
            halves = [(0, P), (P, NG)]
            for q in range(4):
                a, b = halves[q % 2]
                mm = nc.tensor.transpose(psum[0:b - a, 1 + q, 0:P], ext[:, q // 2, a:b], ident[:, :])
            mm.then_inc(s_ext_turned, 1)
            pe.wait_ge(s_pro, 4)
            for q in range(4):
                a, b = halves[q % 2]
                mm = nc.tensor.matmul(psum[:, 5 + q // 2, a:b], ones[0:b - a, :], ext_diag[0:b - a, q, 0:b - a],
                                      start=True, stop=True)
            mm.then_inc(s_ext_spread, 1)

            pe.wait_ge(s_meta, 1)
            pe.reg_mov(summed, 0)
            over_groups(pe, lambda g, k, i: sum_windows(pass1, g, k, i, lambda k, t: rows[:, k, t, :]))

            with pe.Fori(0, NC) as c:
                pe.wait_ge(node1.staged, c + 1)
                pe.wait_ge(node1.copied, c + 1)
                for j in range(C):
                    mm = nc.tensor.transpose(turned[:, j, 0:DA], stage[:, j, :], ident[0:DA, 0:DA])
                mm.then_inc(node1.turned, 1)

            pe.wait_ge(node1.copied, NC + 1)
            pe.reg_mov(summed, 0)
            over_groups(pe, lambda g, k, i: sum_windows(pass2, g, k, i, lambda k, t: rows[:, k, t, :]))

            pe.wait_ge(s_weights, 160)
            with pe.Fori(0, NC) as c:
                pe.wait_ge(node2.staged, c + 1)
                pe.wait_ge(node2.normed, c + 1)
                for j in range(C):
                    mm = nc.tensor.transpose(turned[:, j, 0:DA], stage[:, j, :], ident[0:DA, 0:DA])
                mm.then_inc(node2.turned, 1)
                pe.wait_ge(node2.normed, c + 2)
                for j in range(C):
                    mm = nc.tensor.transpose(turned_x[0:D, j, :], t2[:, j, :], ident[:, :])
                mm.then_inc(node2.x_turned, 1)
                pe.wait_ge(node2.x_staged, 2 * c + 2)
                pe.wait_ge(node2.copied, c + 1)
                for j in range(C):
                    mm = nc.tensor.matmul(hid_ps[:, j, :], stage_x[:, j, :], w_node_sb[:, :], start=True, stop=True)
                mm.then_inc(node2.product, 1)

            def edge_part(g, k, i, free):
                pe.wait_ge(ea_loaded[k], 16 * (i + 1))
                for h in range(2):
                    if free:
                        pe.wait_ge(pre_added, 2 * g + h - 1)
                    for t in range(HALF):
                        mm = nc.tensor.matmul(pre_ps[h][:, t, :],
                                              ea_sb[:, k, h * P:h * P + P], w_edge_sb[:, t, :], start=True, stop=True)
                    mm.then_inc(pre_summed, 1)

            pe.wait_ge(node2.copied, NC + 1)
            pe.reg_mov(summed, 0)
            edge_part(0, 0, 0, False)
            edge_part(1, 1, 0, True)

            def edge_group(g, k, i):
                if not (isinstance(g, int) and g >= NG - 2):
                    edge_part(g + 2, (k + 2) % RING, i + (k + 2) // RING, True)
                sum_windows(pass3, g, k, i, lambda k, t: hid[:, k, t, D:D2 + 1])
            over_groups(pe, edge_group)

            flat_stage = stage[:, :, :].rearrange("f c n -> f (c n)")
            flat_xT = xT[:, :, :].rearrange("f c n -> f (c n)")
            with pe.Fori(0, NC) as c:
                pe.wait_ge(node3.staged, c + 1)
                for q in range(2):
                    mm = nc.tensor.matmul(psum[0:D, q, 0:CN // 2], w_msg2_sb[:, :],
                                          flat_stage[:, q * (CN // 2):(q + 1) * (CN // 2)], start=True, stop=True)
                mm.then_inc(node3.turned, 1)
                pe.wait_ge(node3.x_staged, c + 1)
                for q in range(2):
                    nc.tensor.matmul(psum[0:D, 2 + q, 0:CN // 2], w_upd1x_sb[:, :],
                                     flat_xT[:, bass.ds(c * CN + q * (CN // 2), CN // 2)], start=True, stop=False)
                    mm = nc.tensor.matmul(psum[0:D, 2 + q, 0:CN // 2], w_upd1a_sb[:, :],
                                          aggT[:, q * (CN // 2):(q + 1) * (CN // 2)], start=False, stop=True)
                mm.then_inc(node3.x_turned, 1)
                pe.wait_ge(node3.hidden, c + 1)
                pe.wait_ge(node3.copied, c + 1)
                for j in range(C):
                    mm = nc.tensor.matmul(slots[:, 16 + j, 0:D], updT[:, j * P:(j + 1) * P], w_upd2_sb[:, :],
                                          start=True, stop=True)
                mm.then_inc(node3.product, 1)

        @block.scalar
        def _(act):
            def stage_acc(acc, c):
                view = acc[:, 0:NP].rearrange("f (p t) -> f t p", t=NT)
                return nc.scalar.copy(stage[:, :, :], view[:, bass.ds(c * C, C), :])

            act.wait_ge(pass1.done, 1)
            with act.Fori(0, NC) as c:
                act.wait_ge(node1.turned, c + 1)
                stage_acc(acc_a, c).then_inc(node1.staged, 1)

            act.wait_ge(pass2.done, 1)
            act.wait_ge(node1.turned, NC + 1)
            with act.Fori(0, NC) as c:
                act.wait_ge(node2.turned, c + 1)
                stage_acc(acc_b, c).then_inc(node2.staged, 1)
                act.wait_ge(node2.var, c + 1)
                nc.scalar.activation(col[:, 2, :], col[:, 2, :], ACT.Sqrt).then_inc(node2.std, 1)
                act.wait_ge(node2.x_turned, c + 2)
                nc.scalar.copy(xT[:, bass.ds(c, 1), :].rearrange("f a n -> f (a n)"),
                               psum[0:D, 2:4, :].rearrange("p b n -> p (b n)")[:, 0:CN]).then_inc(node2.x_staged, 1)
                nc.scalar.copy(stage_x[0:D, :, :], turned_x[0:D, :, :]).then_inc(node2.x_staged, 1)
                act.wait_ge(node2.product, c + 1)
                act.wait_ge(node2.stored, 16 * c + 16)
                nc.scalar.copy(hid_nm[:, :, :], hid_ps).then_inc(node2.copied, 1)

            def gelu(g, k):
                for h in range(2):
                    act.wait_ge(pre_added, 2 * g + h + 1)
                    part = hid[:, k, HALF * h:HALF * h + HALF, 0:D2]
                    nc.scalar.activation(part, part, ACT.Gelu).then_inc(hidden_done, 1)

            gelu(0, 0)
            act.wait_ge(s_half_bias, 1)

            def group(g, k, i):
                if not (isinstance(g, int) and g == NG - 1):
                    gelu(g + 1, (k + 1) % RING)
                act.wait_ge(gate_dotted, g + 1)
                nc.scalar.activation(gate_tanh[:, :], gate_dot[:, :], ACT.Tanh, bias=half_b_gate2[:, 0:1],
                                     scale=0.5).then_inc(gate_tanhed, 1)
            over_groups(act, group)

            act.wait_ge(pass3.done, 1)
            with act.Fori(0, NC) as c:
                act.wait_ge(node3.turned, c + 1)
                stage_acc(acc_a, c).then_inc(node3.staged, 1)
                act.wait_ge(node3.turned, c + 2)
                nc.scalar.copy(aggT[:, :].rearrange("f (q n) -> f q n", q=2),
                               psum[0:D, 0:2, 0:CN // 2]).then_inc(node3.x_staged, 1)
                act.wait_ge(node3.x_turned, c + 1)
                act.wait_ge(node3.product, c + 1)
                nc.scalar.activation(updT[0:D, :].rearrange("f (q n) -> f q n", q=2), psum[0:D, 2:4, 0:CN // 2],
                                     ACT.Gelu, bias=b_upd1_sb[:, 0:1]).then_inc(node3.hidden, 1)
                for q in range(2):
                    act.wait_ge(node3.var, 2 * c + q + 1)
                    nc.scalar.activation(col[:, 2, :], col[:, 2, :], ACT.Sqrt).then_inc(node3.std, 1)

        @block.vector
        def _(dve):
            for one in (ones[:, :], rows[:, :, :, D:DA], hid[:, :, :, D2:D2 + 1], stage_x[D:DA, :, :], updT[D:DA, :]):
                last = nc.vector.memset(one, 1.0)
            last.then_inc(s_ones, 1)
            dve.wait_ge(s_ones, 1)
            for ps in (pass1, pass2, pass3):
                for free in (*ps.row_free, ps.here_moved, ps.window_added):
                    dve.sem_inc(free, 1)
            for free in (node1.turned, node1.copied, node2.turned, node2.normed, node2.x_turned, node2.copied,
                         node3.turned, node3.product, node3.copied):
                dve.sem_inc(free, 1)
            dve.sem_inc(node2.stored, 16)

            step, n = steps(dve, s_pro, 0)
            dve.wait_ge(s_dst, 16)
            step(nc.vector.tensor_copy(local[:, :, :].rearrange("p g t -> p (g t)"), dst_i))
            nc.vector.tensor_reduce(ext[:, 0, :], local[:, :, :], AX_X, ALU.max)
            step(nc.vector.tensor_reduce(ext[:, 1, :], local[:, :, :], AX_X, ALU.min, negate=True))
            dve.wait_ge(s_ext_turned, 1)
            parts = [P, NG - P, P, NG - P]
            for q in range(4):
                last = nc.vector.tensor_reduce(ext_red[0:parts[q], q:q + 1], psum[0:parts[q], 1 + q, 0:P], AX_X,
                                               ALU.max)
            step(last)
            for q in range(4):
                last = nc.vector.tensor_scalar(ext_diag[0:parts[q], q, 0:parts[q]], ident[0:parts[q], 0:parts[q]],
                                               ext_red[0:parts[q], q:q + 1], None, ALU.mult)
            step(last)
            dve.wait_ge(s_ext_spread, 1)
            largest, neg_least = psum[:, 5, 0:NG], psum[:, 6, 0:NG]
            step(nc.vector.tensor_copy(first[:, :], neg_least))
            step(nc.vector.tensor_tensor(spread[:, :], largest, first[:, :], ALU.add))
            step(nc.vector.tensor_scalar(wide[:, :], spread[:, :], float(W), None, ALU.is_ge))
            step(nc.vector.tensor_scalar(n_win[:, :], wide[:, :], float(NW - 1), 1.0, ALU.mult, ALU.add))
            step(nc.vector.tensor_scalar(wide[:, :], wide[:, :], -1.0, None, ALU.add))
            step(nc.vector.tensor_tensor(first[:, :], first[:, :], wide[:, :], ALU.mult))
            step(nc.vector.tensor_tensor(local[:, :, :], local[:, :, :],
                                         first[:, :].unsqueeze(2).to_broadcast([P, NG, GT]), ALU.subtract))
            nc.vector.tensor_copy(first_i[:, :], first[0:1, :])
            step(nc.vector.tensor_copy(n_win_i[:, :], n_win[0:1, :]))
            dve.sem_inc(s_meta, 1)
            dve.wait_ge(s_pool_const, 3)
            nc.vector.tensor_copy(iota[:, :], iota_i[:, :])
            nc.vector.memset(acc_a[:, :], 0.0)
            step(nc.vector.memset(acc_b[:, :], 0.0))

            added = dve.alloc_register("dve_windows")
            column = dve.alloc_register("dve_column")

            def add_windows(ps, acc, g, k, gates):
                n = dve.value_load(n_win_i[0:1, bass.ds(g, 1)], min_val=1, max_val=NW)
                base = dve.value_load(first_i[0:1, bass.ds(g, 1)], min_val=0, max_val=N)
                before = dve.snap(added, min_val=0, max_val=NG * NW)
                dve.wait_ge(ps.here_moved, before + 1)
                nc.vector.tensor_scalar(here[:, :], local[:, bass.ds(g, 1), :].rearrange("p g t -> p (g t)"),
                                        0.0, None, ALU.add).then_inc(ps.here_set, 1)
                dve.reg_mov(column, base)
                with dve.Fori(0, n):
                    before = dve.snap(added, min_val=0, max_val=NG * NW)
                    dve.wait_ge(ps.here_set, g + 1)
                    dve.wait_ge(ps.here_moved, before + 1)
                    if gates:
                        dve.wait_ge(gate_set, g + 1)
                        for t in range(GT):
                            last = nc.vector.tensor_scalar(hot[:, t, :], iota[:, :], here[:, t:t + 1],
                                                           gate[:, t:t + 1], ALU.is_equal, ALU.mult)
                    else:
                        last = nc.vector.tensor_tensor(hot[:, :, :], iota[:, :].unsqueeze(1).to_broadcast([P, GT, W]),
                                                       here[:, :].unsqueeze(2).to_broadcast([P, GT, W]), ALU.is_equal)
                    last.then_inc(ps.hot_set, 1)
                    dve.wait_ge(ps.hot_set, before + 1)
                    nc.vector.tensor_scalar(here[:, :], here[:, :], -float(W), None, ALU.add).then_inc(ps.here_moved, 1)
                    dve.wait_ge(ps.window_summed, before + 1)
                    dve.wait_ge(ps.window_added, before + 1)
                    cols = acc[:, bass.ds(dve.snap(column, min_val=0, max_val=AW - W), W)]
                    nc.vector.tensor_tensor(cols, cols, win_ps, ALU.add).then_inc(ps.window_added, 1)
                    dve.reg_add(added, added, 1)
                    dve.reg_add(column, column, W)
                dve.sem_inc(ps.row_free[k], 1)

            def end_pass(ps):
                before = dve.snap(added, min_val=0, max_val=NG * NW)
                dve.wait_ge(ps.window_added, before + 1)
                dve.sem_inc(ps.done, 1)

            dve.reg_mov(added, 0)
            over_groups(dve, lambda g, k, i: add_windows(pass1, acc_a, g, k, False))
            end_pass(pass1)

            def per_feature(a, f=D):
                return a.unsqueeze(2).to_broadcast([P, C, f])

            K1 = 2
            with dve.Fori(0, NC) as c:
                step, n = steps(dve, node1.step, c * K1)
                inv = inv_deg[:, bass.ds(c * C, C)]
                dve.wait_ge(node1.turned, c + 2)
                step(nc.vector.tensor_scalar(col[:, 0, :], turned[:, :, D], 1.0, None, ALU.max))
                step(nc.vector.reciprocal(inv, col[:, 0, :]))
                nc.vector.tensor_tensor(neigh_nm[:, bass.ds(c * C, C), :], turned[:, :, 0:D], per_feature(inv),
                                        ALU.mult).then_inc(node1.copied, 1)
                assert n[0] == K1

            dve.wait_ge(s_weights, 160)
            nc.vector.tensor_scalar(half_b_gate2[:, :], b_gate2_sb[:, :], 0.5, None, ALU.mult).then_inc(s_half_bias, 1)
            nc.vector.memset(acc_a[:, :], 0.0)
            dve.reg_mov(added, 0)
            over_groups(dve, lambda g, k, i: add_windows(pass2, acc_b, g, k, False))
            end_pass(pass2)

            def norm(node, step, src_ap, out_ap, scratch, stds, last_inc):
                mean, var, den, rstd = (col[:, q, :] for q in range(4))
                step(nc.vector.tensor_reduce(mean, src_ap, AX_X, ALU.add))
                step(nc.vector.tensor_scalar(mean, mean, 1.0 / D, None, ALU.mult))
                step(nc.vector.tensor_tensor(out_ap, src_ap, per_feature(mean), ALU.subtract))
                step(nc.vector.tensor_tensor(scratch, out_ap, out_ap, ALU.mult))
                step(nc.vector.tensor_reduce(var, scratch, AX_X, ALU.add))
                nc.vector.tensor_scalar(den, var, 1.0 / D, EPS, ALU.mult, ALU.add).then_inc(node.var, 1)
                dve.wait_ge(node.std, stds)
                step(nc.vector.reciprocal(rstd, den))
                last = nc.vector.tensor_tensor(out_ap, out_ap, per_feature(rstd), ALU.mult)
                last.then_inc(last_inc, 1) if last_inc is not None else step(last)

            K2 = 9
            dve.wait_ge(s_x, 16)
            dve.wait_ge(node1.copied, NC + 1)
            with dve.Fori(0, NC) as c:
                step, n = steps(dve, node2.step, c * K2)
                tiles = bass.ds(c * C, C)
                dve.wait_ge(node2.turned, c + 2)
                step(nc.vector.tensor_tensor(t0[:, :, :], turned[:, :, 0:D], per_feature(inv_deg[:, tiles]), ALU.mult))
                step(nc.vector.tensor_tensor(t1[:, :, :], t0[:, :, :], neigh_nm[:, tiles, :], ALU.add))
                step(nc.vector.scalar_tensor_tensor(out=t0[:, :, :], in0=t1[:, :, :], scalar=0.5,
                                                    in1=x_nm[:, tiles, :], op0=ALU.mult, op1=ALU.add))
                dve.wait_ge(node2.x_turned, c + 1)
                norm(node2, step, t0[:, :, :], t2[:, :, :], t1[:, :, :], c + 1, node2.normed)
                dve.wait_ge(node2.normed, c + 2)
                nc.vector.tensor_scalar(x_nm[:, tiles, :], t2[:, :, :], 0.0, None, ALU.add).then_inc(node2.hidden, 1)
                assert n[0] == K2, n

            dve.reg_mov(added, 0)

            def add_node_part(g, k, i):
                dve.wait_ge(pass3.gathered[k], 16 * GT * (i + 1))
                for h in range(2):
                    dve.wait_ge(pre_summed, 2 * g + h + 1)
                    part = hid[:, k, HALF * h:HALF * h + HALF, 0:D2]
                    nc.vector.tensor_tensor(part, part, pre_ps[h], ALU.add).then_inc(pre_added, 1)

            add_node_part(0, 0, 0)

            def group(g, k, i):
                if not (isinstance(g, int) and g == NG - 1):
                    add_node_part(g + 1, (k + 1) % RING, i + (k + 1) // RING)
                dve.wait_ge(hidden_done, 2 * g + 2)
                nc.vector.tensor_tensor(prod[:, :, :], hid[:, k, :, 0:D],
                                        w_gate2_sb[:, :].unsqueeze(1).to_broadcast([P, GT, D]), ALU.mult)\
                    .then_inc(gate_prod, 1)
                dve.wait_ge(gate_prod, g + 1)
                nc.vector.tensor_reduce(gate_dot[:, :], prod[:, :, :], AX_X, ALU.add).then_inc(gate_dotted, 1)
                dve.wait_ge(gate_tanhed, g + 1)
                nc.vector.tensor_scalar(gate[:, :], gate_tanh[:, :], 0.5, 0.5, ALU.mult, ALU.add).then_inc(gate_set, 1)
                add_windows(pass3, acc_a, g, k, True)
            over_groups(dve, group)
            end_pass(pass3)

            K3 = 16
            dve.wait_ge(node2.hidden, NC)
            with dve.Fori(0, NC) as c:
                step, n = steps(dve, node3.step, c * K3)
                tiles = bass.ds(c * C, C)
                dve.wait_ge(node3.product, c + 2)
                nc.vector.tensor_tensor(t0[:, :, :], slots[:, 16:16 + C, 0:D], x_nm[:, tiles, :], ALU.add)\
                    .then_inc(node3.copied, 1)
                dve.wait_ge(node3.copied, c + 2)
                norm(node3, step, t0[:, :, :], t2[:, :, :], t1[:, :, :], 2 * c + 1, None)
                gain, shift = (ln_gb_sb[:, q * D:q * D + D].unsqueeze(1).to_broadcast([P, C, D]) for q in range(2))
                step(nc.vector.tensor_tensor(t0[:, :, :], t2[:, :, :], gain, ALU.mult))
                step(nc.vector.tensor_tensor(t1[:, :, :], t0[:, :, :], shift, ALU.add))
                step(nc.vector.tensor_tensor(t0[:, :, :], t1[:, :, :], x_nm[:, tiles, :], ALU.add))
                norm(node3, step, t0[:, :, :], out_nm[:, tiles, :], t1[:, :, :], 2 * c + 2, node3.normed)
                assert n[0] == K3, n


def kernel(x, src, dst, edge_attr_32, L1_gnn_mW1, L1_gnn_mb1, L1_gnn_mW2, L1_gnn_mb2, L1_gnn_gW1, L1_gnn_gb1,
           L1_gnn_gW2, L1_gnn_gb2, L1_gnn_uW1, L1_gnn_ub1, L1_gnn_uW2, L1_gnn_ub2, L1_gnn_ln_g, L1_gnn_ln_b):
    import numpy as np
    import concourse.bacc as bacc
    from concourse.bass_utils import run_bass_kernel_spmd

    (x, src, dst, ea, mW1, mb1, mW2, mb2, gW1, gb1, gW2, gb2, uW1, ub1, uW2, ub2, ln_g, ln_b) = (
        np.asarray(a) for a in (
            x, src, dst, edge_attr_32, L1_gnn_mW1, L1_gnn_mb1, L1_gnn_mW2, L1_gnn_mb2, L1_gnn_gW1, L1_gnn_gb1,
            L1_gnn_gW2, L1_gnn_gb2, L1_gnn_uW1, L1_gnn_ub1, L1_gnn_uW2, L1_gnn_ub2, L1_gnn_ln_g, L1_gnn_ln_b))
    pad = NG * GE - E

    def rows_of(*parts):
        return np.concatenate([p.reshape(-1, p.shape[-1]) for p in parts], axis=0)

    src_l = np.concatenate([src, np.zeros(pad, src.dtype)]).reshape(NG, GT, P)
    dst_l = np.concatenate([dst, np.full(pad, N, dst.dtype)]).reshape(NG, GT, P)
    ea_l = np.concatenate([ea, np.zeros((pad, DE), ea.dtype)]).reshape(NG, 2, HALF, P, DE)
    node_w = np.concatenate([rows_of(gW1[:D], gb1), rows_of(mW1[:D], mb1)], axis=1)
    edge_w = np.concatenate([gW1[D:], mW1[D:]], axis=1)
    edge_w_apart = np.zeros((HALF, DE, HALF, D2), edge_w.dtype)
    for t in range(HALF):
        edge_w_apart[t, :, t] = edge_w
    ins = {
        "x": np.concatenate([x, np.zeros((NP - N, D), x.dtype)]).reshape(P, NT * D),
        "src": src_l.transpose(0, 2, 1),
        "dst": dst_l.transpose(2, 0, 1).reshape(P, NG * GT),
        "ea": ea_l.transpose(0, 2, 4, 1, 3).reshape(NG, P, 2 * P),
        "w_node": node_w,
        "w_edge": edge_w_apart.reshape(P, HALF * D2),
        "w_msg2": rows_of(mW2, mb2),
        "w_gate2": np.tile(gW2.reshape(1, D), (P, 1)),
        "b_gate2": np.tile(gb2.reshape(1, 1), (P, 1)),
        "w_upd1x": uW1[:D],
        "w_upd1a": uW1[D:],
        "b_upd1": ub1.reshape(D, 1),
        "w_upd2": rows_of(uW2, ub2),
        "ln_gb": np.tile(np.concatenate([ln_g, ln_b]).reshape(1, 2 * D), (P, 1)),
    }
    nc = bacc.Bacc("TRN2", target_bir_lowering=False, num_devices=1)
    arrays, args = {}, []
    for name, a in ins.items():
        a = np.ascontiguousarray(a)
        arrays[f"in_{name}"] = a
        args.append(nc.dram_tensor(f"in_{name}", a.shape, mybir.dt.from_np(a.dtype), kind="ExternalInput").ap())
    args.append(nc.dram_tensor("out_nodes", (P, NT * D), F32, kind="ExternalOutput").ap())
    bass_gnn(nc, *args)
    r = run_bass_kernel_spmd(nc, [arrays], core_ids=[0])
    return r.results[0]["out_nodes"].reshape(NP, D)[:N]
```

```python
from contextlib import ExitStack

import concourse.bass as bass
from concourse import mybir

ALU = mybir.AluOpType
ACT = mybir.ActivationFunctionType
F32 = mybir.dt.float32
I32 = mybir.dt.int32
U32 = mybir.dt.uint32
AX_X = mybir.AxisListType.X

P = 128
N, E, D, DE = 6250, 206250, 96, 32
NT = -(-N // P)
NP = NT * P
GT = 8
GE = GT * P
NG = -(-E // GE)
RING = 4
ROUNDS = NG // RING
W = 64
NW = -(-(N + 1) // W)
AW = NP + W
DA = D + 1
D2 = 2 * D
C = 7
NC = NT // C
CN = C * P
HALF = GT // 2
EPS = 1e-5

assert NC * C == NT and (NG * GE - E) < GE and NW * W <= AW


def bass_gnn(nc, x, src, dst, ea, w_node, w_edge, w_msg2, w_gate2, b_gate2, w_upd1x, w_upd1a, b_upd1,
             w_upd2, ln_gb, out):
    neigh_table = nc.dram_tensor("neigh_table", [NP, D], F32, kind="Internal").ap()
    hidden_table = nc.dram_tensor("hidden_table", [NP, D2], F32, kind="Internal").ap()
    x_table = x.rearrange("p (t f) -> (p t) f", f=D)

    with ExitStack() as ctx:
        def sb(name, shape, dt=F32):
            return ctx.enter_context(nc.sbuf_tensor(name, shape, dt))

        def sem(name):
            return ctx.enter_context(nc.semaphore(name))

        ident = sb("ident", [P, P])
        iota_i = sb("iota_i", [P, W], I32)
        iota = sb("iota", [P, W])
        ones = sb("ones", [P, P])
        w_node_sb = sb("w_node_sb", [DA, D2])
        w_edge_sb = sb("w_edge_sb", [P, HALF, D2])
        w_msg2_sb = sb("w_msg2_sb", [DA, D])
        w_gate2_sb = sb("w_gate2_sb", [P, D])
        b_gate2_sb = sb("b_gate2_sb", [P, 1])
        half_b_gate2 = sb("half_b_gate2", [P, 1])
        w_upd1x_sb = sb("w_upd1x_sb", [D, D])
        w_upd1a_sb = sb("w_upd1a_sb", [D, D])
        b_upd1_sb = sb("b_upd1_sb", [D, 1])
        w_upd2_sb = sb("w_upd2_sb", [DA, D])
        ln_gb_sb = sb("ln_gb_sb", [P, 2 * D])

        local = sb("local", [P, NG, GT])
        ext = sb("ext", [P, 2, NG])
        ext_red = sb("ext_red", [P, 4])
        spread = sb("spread", [P, NG])
        wide = sb("wide", [P, NG])
        first = sb("first", [P, NG])
        n_win = sb("n_win", [P, NG])
        first_i = sb("first_i", [1, NG], I32)
        n_win_i = sb("n_win_i", [1, NG], I32)

        idx = sb("idx", [P, RING, GT], I32)
        rows = sb("rows", [P, RING, GT, DA])
        hid = sb("hid", [P, RING, GT, D2 + 1])
        ea_sb = sb("ea_sb", [P, RING, 2 * P])
        here = sb("here", [P, GT])
        hot = sb("hot", [P, GT, W])
        hot01 = sb("hot01", [P, GT, W])
        prod = sb("prod", [P, GT, D])
        ext_diag = prod[:, :, :].rearrange("p t f -> p (t f)")[:, 0:4 * P].rearrange("p (q n) -> p q n", q=4)
        gate_dot = sb("gate_dot", [P, GT])
        gate_tanh = sb("gate_tanh", [P, GT])
        gate = sb("gate", [P, GT])
        acc_a = sb("acc_a", [DA, AW])
        acc_b = sb("acc_b", [DA, AW])

        x_nm = sb("x_nm", [P, NT, D])
        neigh_nm = sb("neigh_nm", [P, NT, D])
        dst_i = neigh_nm[:, :, :].rearrange("p t f -> p (t f)")[:, 0:NG * GT].bitcast(I32)
        inv_deg = sb("inv_deg", [P, NT])
        xT = sb("xT", [D, NC, CN])
        stage = sb("stage", [DA, C, P])
        stage_x = sb("stage_x", [DA, C, P])
        aggT = sb("aggT", [D, CN])
        updT = sb("updT", [DA, CN])
        t0 = sb("t0", [P, C, D])
        t1 = sb("t1", [P, C, D])
        t2 = sb("t2", [P, C, D])
        col = sb("col", [P, 4, C])
        hid_nm = sb("hid_nm", [P, C, D2])
        out_nm = neigh_nm

        psum = ctx.enter_context(nc.psum_tensor("psum", [P, 8, 512], F32))
        win_ps = psum[0:DA, 0, 0:W]
        pre_ps = [psum[:, 1 + 2 * h:3 + 2 * h, :].rearrange("p b (t n) -> p (b t) n", t=2)[:, :, 0:D2]
                  for h in range(2)]
        slots = psum[:, :, :].rearrange("p b (s n) -> p (b s) n", n=P)
        turned = slots[:, 0:C, :]
        turned_x = slots[:, 8:8 + C, :]
        hid_ps = psum[:, 4:8, :].rearrange("p b (t n) -> p (b t) n", t=2)[:, 0:C, 0:D2]

        s_weights = sem("s_weights")
        s_dst = sem("s_dst")
        s_x = sem("s_x")
        s_pool_const = sem("s_pool_const")
        s_pro = sem("s_pro")
        s_ext_turned = sem("s_ext_turned")
        s_ext_spread = sem("s_ext_spread")
        s_meta = sem("s_meta")
        s_ones = sem("s_ones")
        s_half_bias = sem("s_half_bias")

        class EdgePass:
            def __init__(self, name):
                self.idx_loaded = [sem(f"{name}_idx_loaded{k}") for k in range(RING)]
                self.gathered = [sem(f"{name}_gathered{k}") for k in range(RING)]
                self.row_free = [sem(f"{name}_row_free{k}") for k in range(RING)]
                self.matched = sem(f"{name}_matched")
                self.hot_set = sem(f"{name}_hot_set")
                self.window_summed = sem(f"{name}_window_summed")
                self.window_added = sem(f"{name}_window_added")
                self.here_set = sem(f"{name}_here_set")
                self.here_moved = sem(f"{name}_here_moved")
                self.more_matched = sem(f"{name}_more_matched")
                self.more_hot_set = sem(f"{name}_more_hot_set")
                self.more_summed = sem(f"{name}_more_summed")
                self.more_added = sem(f"{name}_more_added")
                self.done = sem(f"{name}_done")

        pass1, pass2, pass3 = EdgePass("p1"), EdgePass("p2"), EdgePass("p3")
        ea_loaded = [sem(f"ea_loaded{k}") for k in range(RING)]
        pre_summed = sem("pre_summed")
        pre_added = sem("pre_added")
        hidden_done = sem("hidden_done")
        gate_prod = sem("gate_prod")
        gate_dotted = sem("gate_dotted")
        gate_tanhed = sem("gate_tanhed")
        gate_set = sem("gate_set")

        class NodePhase:
            def __init__(self, name):
                self.staged = sem(f"{name}_staged")
                self.turned = sem(f"{name}_turned")
                self.step = sem(f"{name}_step")
                self.var = sem(f"{name}_var")
                self.std = sem(f"{name}_std")
                self.normed = sem(f"{name}_normed")
                self.x_turned = sem(f"{name}_x_turned")
                self.x_staged = sem(f"{name}_x_staged")
                self.product = sem(f"{name}_product")
                self.copied = sem(f"{name}_copied")
                self.hidden = sem(f"{name}_hidden")
                self.stored = sem(f"{name}_stored")

        node1, node2, node3 = NodePhase("n1"), NodePhase("n2"), NodePhase("n3")

        block = ctx.enter_context(nc.Block())

        def steps(eng, sem_, base):
            n = [0]

            def step(ins):
                n[0] += 1
                ins.then_inc(sem_, 1)
                eng.wait_ge(sem_, base + n[0])
            return step, n

        def over_groups(eng, body, last=NG):
            with eng.Fori(0, last // RING) as i:
                for k in range(RING):
                    body(i * RING + k, k, i)
            for g in range(last // RING * RING, last):
                body(g, g % RING, g // RING)

        @block.sync
        def _(sp):
            def load_idx(ps, g, k):
                sp.dma_start(idx[:, k, :], src[bass.ds(g, 1), :, :].rearrange("g p t -> (g p) t")).then_inc(
                    ps.idx_loaded[k], 16)

            def load_ea(g, k):
                sp.dma_start(ea_sb[:, k, :], ea[bass.ds(g, 1), :, :].rearrange("g p n -> (g p) n")).then_inc(
                    ea_loaded[k], 16)

            for k in range(RING):
                load_idx(pass1, k, k)
            sp.dma_start(dst_i, dst).then_inc(s_dst, 16)
            for to, of in ((w_node_sb[:, :], w_node), (w_edge_sb[:, :, :].rearrange("p t n -> p (t n)"), w_edge), (w_msg2_sb[:, :], w_msg2), (w_gate2_sb[:, :], w_gate2),
                           (b_gate2_sb[:, :], b_gate2), (w_upd1x_sb[:, :], w_upd1x), (w_upd1a_sb[:, :], w_upd1a),
                           (b_upd1_sb[:, :], b_upd1), (w_upd2_sb[:, :], w_upd2), (ln_gb_sb[:, :], ln_gb)):
                sp.dma_start(to, of).then_inc(s_weights, 16)
            sp.dma_start(x_nm[:, :, :].rearrange("p t f -> p (t f)"), x).then_inc(s_x, 16)

            def feed(ps):
                def refill(g, k, i):
                    sp.wait_ge(ps.gathered[k], 16 * GT * (i + 1))
                    load_idx(ps, g + RING, k)
                over_groups(sp, refill, NG - RING)

            def store_table(node, table, of, f):
                view = table.rearrange("(p t) f -> p (t f)", p=P)
                with sp.Fori(0, NC) as c:
                    sp.wait_ge(node.copied, c + 2)
                    sp.dma_start(view[:, bass.ds(c * (C * f), C * f)], of(c)).then_inc(node.stored, 16)

            feed(pass1)
            for k in range(RING):
                sp.wait_ge(pass1.gathered[k], 16 * GT * len(range(k, NG, RING)))
                load_idx(pass2, k, k)
            flat = neigh_nm[:, :, :].rearrange("p t f -> p (t f)")
            store_table(node1, neigh_table, lambda c: flat[:, bass.ds(c * (C * D), C * D)], D)
            feed(pass2)
            for k in range(RING):
                sp.wait_ge(pass2.gathered[k], 16 * GT * len(range(k, NG, RING)))
                load_idx(pass3, k, k)
                load_ea(k, k)
            with sp.Fori(0, NC) as c:
                sp.wait_ge(node2.copied, c + 2)
                sp.dma_start(hidden_table.rearrange("(p t) f -> p (t f)", p=P)[:, bass.ds(c * (C * D2), C * D2)],
                             hid_nm[:, :, :].rearrange("p t f -> p (t f)")).then_inc(node2.stored, 16)

            def refill3(g, k, i):
                sp.wait_ge(pass3.gathered[k], 16 * GT * (i + 1))
                load_idx(pass3, g + RING, k)
                sp.wait_ge(pre_summed, 2 * g + 2)
                load_ea(g + RING, k)
            over_groups(sp, refill3, NG - RING)

            with sp.Fori(0, NC) as c:
                sp.wait_ge(node3.normed, c + 1)
                sp.dma_start(out[:, bass.ds(c * (C * D), C * D)],
                             out_nm[:, :, :].rearrange("p t f -> p (t f)")[:, bass.ds(c * (C * D), C * D)]).then_inc(
                    node3.stored, 16)
            sp.wait_ge(node3.stored, 16 * NC)

        @block.gpsimd
        def _(pool):
            nc.gpsimd.memset(ident[:], 0.0).then_inc(s_pool_const, 1)
            nc.gpsimd.iota(iota_i[:], pattern=[[1, W]], base=0, channel_multiplier=0).then_inc(s_pool_const, 1)
            pool.wait_ge(s_pool_const, 2)
            nc.gpsimd.affine_select(out=ident[:], in_=ident[:], compare_op=ALU.not_equal, fill=1.0, base=0,
                                    pattern=[[-1, P]], channel_multiplier=1).then_inc(s_pool_const, 1)

            def gather_all(ps, table, buf, width):
                def gather(g, k, i):
                    pool.wait_ge(ps.idx_loaded[k], 16 * (i + 1))
                    pool.wait_ge(ps.row_free[k], i + 1)
                    pool.nop(nofuse=True)
                    for t in range(GT):
                        pool.indirect_dma_start(
                            buf[:, k, t, 0:width], None, table,
                            bass.IndirectOffsetOnAxis(ap=idx[:, k, t:t + 1].bitcast(U32), axis=0),
                        ).then_inc(ps.gathered[k], 16)
                over_groups(pool, gather)

            gather_all(pass1, x_table, rows, D)
            pool.wait_ge(node1.stored, 16 * NC)
            gather_all(pass2, neigh_table, rows, D)
            pool.wait_ge(node2.stored, 16 * (NC + 1))
            gather_all(pass3, hidden_table, hid, D2)

        @block.tensor
        def _(pe):
            more = pe.alloc_register("pe_more_windows")

            def sum_windows(ps, g, k, i, rhs_rows):
                n = pe.value_load(n_win_i[0:1, bass.ds(g, 1)], min_val=1, max_val=NW)
                pe.wait_ge(ps.gathered[k], 16 * GT * (i + 1))
                if ps is pass3:
                    pe.wait_ge(hidden_done, 2 * g + 2)
                pe.wait_ge(ps.hot_set, g + 1)
                for t in range(GT):
                    mm = nc.tensor.matmul(win_ps, rhs_rows(k, t), hot[:, t, :], start=(t == 0), stop=(t == GT - 1))
                mm.then_inc(ps.window_summed, 1)
                with pe.If(n > 1):
                    with pe.Fori(1, n):
                        pe.wait_ge(ps.more_hot_set, pe.snap(more, min_val=0, max_val=NG * NW) + 1)
                        for t in range(GT):
                            mm = nc.tensor.matmul(win_ps, rhs_rows(k, t), hot[:, t, :], start=(t == 0),
                                                  stop=(t == GT - 1))
                        mm.then_inc(ps.more_summed, 1)
                        pe.reg_add(more, more, 1)

            pe.wait_ge(s_pool_const, 3)
            pe.wait_ge(s_pro, 2)
            halves = [(0, P), (P, NG)]
            for q in range(4):
                a, b = halves[q % 2]
                mm = nc.tensor.transpose(psum[0:b - a, 1 + q, 0:P], ext[:, q // 2, a:b], ident[:, :])
            mm.then_inc(s_ext_turned, 1)
            pe.wait_ge(s_pro, 4)
            for q in range(4):
                a, b = halves[q % 2]
                mm = nc.tensor.matmul(psum[:, 5 + q // 2, a:b], ones[0:b - a, :], ext_diag[0:b - a, q, 0:b - a],
                                      start=True, stop=True)
            mm.then_inc(s_ext_spread, 1)

            pe.wait_ge(s_meta, 1)
            pe.reg_mov(more, 0)
            over_groups(pe, lambda g, k, i: sum_windows(pass1, g, k, i, lambda k, t: rows[:, k, t, :]))

            with pe.Fori(0, NC) as c:
                pe.wait_ge(node1.staged, c + 1)
                pe.wait_ge(node1.copied, c + 1)
                for j in range(C):
                    mm = nc.tensor.transpose(turned[:, j, 0:DA], stage[:, j, :], ident[0:DA, 0:DA])
                mm.then_inc(node1.turned, 1)

            pe.wait_ge(node1.copied, NC + 1)
            pe.reg_mov(more, 0)
            over_groups(pe, lambda g, k, i: sum_windows(pass2, g, k, i, lambda k, t: rows[:, k, t, :]))

            pe.wait_ge(s_weights, 160)
            with pe.Fori(0, NC) as c:
                pe.wait_ge(node2.staged, c + 1)
                pe.wait_ge(node2.normed, c + 1)
                for j in range(C):
                    mm = nc.tensor.transpose(turned[:, j, 0:DA], stage[:, j, :], ident[0:DA, 0:DA])
                mm.then_inc(node2.turned, 1)
                pe.wait_ge(node2.normed, c + 2)
                for j in range(C):
                    mm = nc.tensor.transpose(turned_x[0:D, j, :], t2[:, j, :], ident[:, :])
                mm.then_inc(node2.x_turned, 1)
                pe.wait_ge(node2.x_staged, 2 * c + 2)
                pe.wait_ge(node2.copied, c + 1)
                for j in range(C):
                    mm = nc.tensor.matmul(hid_ps[:, j, :], stage_x[:, j, :], w_node_sb[:, :], start=True, stop=True)
                mm.then_inc(node2.product, 1)

            def edge_part(g, k, i, free):
                pe.wait_ge(ea_loaded[k], 16 * (i + 1))
                for h in range(2):
                    if free:
                        pe.wait_ge(pre_added, 2 * g + h - 1)
                    for t in range(HALF):
                        mm = nc.tensor.matmul(pre_ps[h][:, t, :],
                                              ea_sb[:, k, h * P:h * P + P], w_edge_sb[:, t, :], start=True, stop=True)
                    mm.then_inc(pre_summed, 1)

            pe.wait_ge(node2.copied, NC + 1)
            pe.reg_mov(more, 0)
            edge_part(0, 0, 0, False)
            edge_part(1, 1, 0, True)

            def edge_group(g, k, i):
                if not (isinstance(g, int) and g >= NG - 2):
                    edge_part(g + 2, (k + 2) % RING, i + (k + 2) // RING, True)
                sum_windows(pass3, g, k, i, lambda k, t: hid[:, k, t, D:D2 + 1])
            over_groups(pe, edge_group)

            flat_stage = stage[:, :, :].rearrange("f c n -> f (c n)")
            flat_xT = xT[:, :, :].rearrange("f c n -> f (c n)")
            with pe.Fori(0, NC) as c:
                pe.wait_ge(node3.staged, c + 1)
                for q in range(2):
                    mm = nc.tensor.matmul(psum[0:D, q, 0:CN // 2], w_msg2_sb[:, :],
                                          flat_stage[:, q * (CN // 2):(q + 1) * (CN // 2)], start=True, stop=True)
                mm.then_inc(node3.turned, 1)
                pe.wait_ge(node3.x_staged, c + 1)
                for q in range(2):
                    nc.tensor.matmul(psum[0:D, 2 + q, 0:CN // 2], w_upd1x_sb[:, :],
                                     flat_xT[:, bass.ds(c * CN + q * (CN // 2), CN // 2)], start=True, stop=False)
                    mm = nc.tensor.matmul(psum[0:D, 2 + q, 0:CN // 2], w_upd1a_sb[:, :],
                                          aggT[:, q * (CN // 2):(q + 1) * (CN // 2)], start=False, stop=True)
                mm.then_inc(node3.x_turned, 1)
                pe.wait_ge(node3.hidden, c + 1)
                pe.wait_ge(node3.copied, c + 1)
                for j in range(C):
                    mm = nc.tensor.matmul(slots[:, 16 + j, 0:D], updT[:, j * P:(j + 1) * P], w_upd2_sb[:, :],
                                          start=True, stop=True)
                mm.then_inc(node3.product, 1)

        @block.scalar
        def _(act):
            def stage_acc(acc, c):
                view = acc[:, 0:NP].rearrange("f (p t) -> f t p", t=NT)
                return nc.scalar.copy(stage[:, :, :], view[:, bass.ds(c * C, C), :])

            act.wait_ge(pass1.done, 1)
            with act.Fori(0, NC) as c:
                act.wait_ge(node1.turned, c + 1)
                stage_acc(acc_a, c).then_inc(node1.staged, 1)

            act.wait_ge(pass2.done, 1)
            act.wait_ge(node1.turned, NC + 1)
            with act.Fori(0, NC) as c:
                act.wait_ge(node2.turned, c + 1)
                stage_acc(acc_b, c).then_inc(node2.staged, 1)
                act.wait_ge(node2.var, c + 1)
                nc.scalar.activation(col[:, 2, :], col[:, 2, :], ACT.Sqrt).then_inc(node2.std, 1)
                act.wait_ge(node2.x_turned, c + 2)
                nc.scalar.copy(xT[:, bass.ds(c, 1), :].rearrange("f a n -> f (a n)"),
                               psum[0:D, 2:4, :].rearrange("p b n -> p (b n)")[:, 0:CN]).then_inc(node2.x_staged, 1)
                nc.scalar.copy(stage_x[0:D, :, :], turned_x[0:D, :, :]).then_inc(node2.x_staged, 1)
                act.wait_ge(node2.product, c + 1)
                act.wait_ge(node2.stored, 16 * c + 16)
                nc.scalar.copy(hid_nm[:, :, :], hid_ps).then_inc(node2.copied, 1)

            def gelu(g, k):
                for h in range(2):
                    act.wait_ge(pre_added, 2 * g + h + 1)
                    part = hid[:, k, HALF * h:HALF * h + HALF, 0:D2]
                    nc.scalar.activation(part, part, ACT.Gelu).then_inc(hidden_done, 1)

            def tanh(g):
                act.wait_ge(gate_dotted, g + 1)
                nc.scalar.activation(gate_tanh[:, :], gate_dot[:, :], ACT.Tanh, bias=half_b_gate2[:, 0:1],
                                     scale=0.5).then_inc(gate_tanhed, 1)

            act.wait_ge(s_half_bias, 1)
            gelu(0, 0)
            gelu(1, 1)
            tanh(0)

            def group(g, k, i):
                last = g if isinstance(g, int) else 0
                if last < NG - 2:
                    gelu(g + 2, (k + 2) % RING)
                if last < NG - 1:
                    tanh(g + 1)
            over_groups(act, group)

            act.wait_ge(pass3.done, 1)
            with act.Fori(0, NC) as c:
                act.wait_ge(node3.turned, c + 1)
                stage_acc(acc_a, c).then_inc(node3.staged, 1)
                act.wait_ge(node3.turned, c + 2)
                nc.scalar.copy(aggT[:, :].rearrange("f (q n) -> f q n", q=2),
                               psum[0:D, 0:2, 0:CN // 2]).then_inc(node3.x_staged, 1)
                act.wait_ge(node3.x_turned, c + 1)
                act.wait_ge(node3.product, c + 1)
                nc.scalar.activation(updT[0:D, :].rearrange("f (q n) -> f q n", q=2), psum[0:D, 2:4, 0:CN // 2],
                                     ACT.Gelu, bias=b_upd1_sb[:, 0:1]).then_inc(node3.hidden, 1)
                for q in range(2):
                    act.wait_ge(node3.var, 2 * c + q + 1)
                    nc.scalar.activation(col[:, 2, :], col[:, 2, :], ACT.Sqrt).then_inc(node3.std, 1)

        @block.vector
        def _(dve):
            for one in (ones[:, :], rows[:, :, :, D:DA], hid[:, :, :, D2:D2 + 1], stage_x[D:DA, :, :], updT[D:DA, :]):
                last = nc.vector.memset(one, 1.0)
            last.then_inc(s_ones, 1)
            dve.wait_ge(s_ones, 1)
            for ps in (pass1, pass2, pass3):
                for free in (*ps.row_free, ps.window_added, ps.more_added):
                    dve.sem_inc(free, 1)
            for free in (node1.turned, node1.copied, node2.turned, node2.normed, node2.x_turned, node2.copied,
                         node3.turned, node3.product, node3.copied):
                dve.sem_inc(free, 1)
            dve.sem_inc(node2.stored, 16)

            step, n = steps(dve, s_pro, 0)
            dve.wait_ge(s_dst, 16)
            step(nc.vector.tensor_copy(local[:, :, :].rearrange("p g t -> p (g t)"), dst_i))
            nc.vector.tensor_reduce(ext[:, 0, :], local[:, :, :], AX_X, ALU.max)
            step(nc.vector.tensor_reduce(ext[:, 1, :], local[:, :, :], AX_X, ALU.min, negate=True))
            dve.wait_ge(s_ext_turned, 1)
            parts = [P, NG - P, P, NG - P]
            for q in range(4):
                last = nc.vector.tensor_reduce(ext_red[0:parts[q], q:q + 1], psum[0:parts[q], 1 + q, 0:P], AX_X,
                                               ALU.max)
            step(last)
            for q in range(4):
                last = nc.vector.tensor_scalar(ext_diag[0:parts[q], q, 0:parts[q]], ident[0:parts[q], 0:parts[q]],
                                               ext_red[0:parts[q], q:q + 1], None, ALU.mult)
            step(last)
            dve.wait_ge(s_ext_spread, 1)
            largest, neg_least = psum[:, 5, 0:NG], psum[:, 6, 0:NG]
            step(nc.vector.tensor_copy(first[:, :], neg_least))
            step(nc.vector.tensor_tensor(spread[:, :], largest, first[:, :], ALU.add))
            step(nc.vector.tensor_scalar(wide[:, :], spread[:, :], float(W), None, ALU.is_ge))
            step(nc.vector.tensor_scalar(n_win[:, :], wide[:, :], float(NW - 1), 1.0, ALU.mult, ALU.add))
            step(nc.vector.tensor_scalar(wide[:, :], wide[:, :], -1.0, None, ALU.add))
            step(nc.vector.tensor_tensor(first[:, :], first[:, :], wide[:, :], ALU.mult))
            step(nc.vector.tensor_tensor(local[:, :, :], local[:, :, :],
                                         first[:, :].unsqueeze(2).to_broadcast([P, NG, GT]), ALU.subtract))
            nc.vector.tensor_copy(first_i[:, :], first[0:1, :])
            step(nc.vector.tensor_copy(n_win_i[:, :], n_win[0:1, :]))
            dve.sem_inc(s_meta, 1)
            dve.wait_ge(s_pool_const, 3)
            nc.vector.tensor_copy(iota[:, :], iota_i[:, :])
            nc.vector.memset(acc_a[:, :], 0.0)
            step(nc.vector.memset(acc_b[:, :], 0.0))

            more = dve.alloc_register("dve_more_windows")
            wides = dve.alloc_register("dve_wide_groups")
            column = dve.alloc_register("dve_column")
            over_tiles = iota[:, :].unsqueeze(1).to_broadcast([P, GT, W])

            def over_window(a):
                return a.unsqueeze(2).to_broadcast([P, GT, W])

            def match(ps, g):
                to = hot01 if ps is pass3 else hot
                nc.vector.tensor_tensor(to[:, :, :], over_tiles,
                                        over_window(local[:, bass.ds(g, 1), :].rearrange("p g t -> p (g t)")),
                                        ALU.is_equal).then_inc(ps.matched if ps is pass3 else ps.hot_set, 1)

            def add_windows(ps, acc, g, k):
                n = dve.value_load(n_win_i[0:1, bass.ds(g, 1)], min_val=1, max_val=NW)
                base = dve.value_load(first_i[0:1, bass.ds(g, 1)], min_val=0, max_val=N)
                dve.wait_ge(ps.window_summed, g + 1)
                dve.wait_ge(ps.window_added, g + 1)
                cols = acc[:, bass.ds(base, W)]
                nc.vector.tensor_tensor(cols, cols, win_ps, ALU.add).then_inc(ps.window_added, 1)
                with dve.If(n > 1):
                    nc.vector.tensor_scalar(here[:, :], local[:, bass.ds(g, 1), :].rearrange("p g t -> p (g t)"),
                                            0.0, None, ALU.add).then_inc(ps.here_set, 1)
                    dve.reg_mov(column, W)
                    with dve.Fori(1, n):
                        before = dve.snap(more, min_val=0, max_val=NG * NW)
                        dve.wait_ge(ps.here_set, dve.snap(wides, min_val=0, max_val=NG) + 1)
                        dve.wait_ge(ps.more_added, before + 1)
                        nc.vector.tensor_scalar(here[:, :], here[:, :], -float(W), None, ALU.add)\
                            .then_inc(ps.here_moved, 1)
                        dve.wait_ge(ps.here_moved, before + 1)
                        nc.vector.tensor_tensor(hot[:, :, :], over_tiles, over_window(here[:, :]), ALU.is_equal)\
                            .then_inc(ps.more_matched, 1)
                        dve.wait_ge(ps.more_matched, before + 1)
                        factor = over_window(gate[:, :]) if ps is pass3 else hot[:, :, :]
                        nc.vector.tensor_tensor(hot[:, :, :], hot[:, :, :], factor, ALU.mult)\
                            .then_inc(ps.more_hot_set, 1)
                        dve.wait_ge(ps.more_summed, before + 1)
                        dve.wait_ge(ps.window_added, g + 2)
                        cols = acc[:, bass.ds(dve.snap(column, min_val=0, max_val=AW - W), W)]
                        nc.vector.tensor_tensor(cols, cols, win_ps, ALU.add).then_inc(ps.more_added, 1)
                        dve.reg_add(more, more, 1)
                        dve.reg_add(column, column, W)
                    dve.reg_add(wides, wides, 1)
                dve.sem_inc(ps.row_free[k], 1)

            def end_pass(ps):
                dve.wait_ge(ps.window_added, NG + 1)
                dve.wait_ge(ps.more_added, dve.snap(more, min_val=0, max_val=NG * NW) + 1)
                dve.sem_inc(ps.done, 1)

            def mean_pass(ps, acc):
                for register in (more, wides):
                    dve.reg_mov(register, 0)
                match(ps, 0)

                def group(g, k, i):
                    add_windows(ps, acc, g, k)
                    if not (isinstance(g, int) and g == NG - 1):
                        match(ps, g + 1)
                over_groups(dve, group)
                end_pass(ps)

            mean_pass(pass1, acc_a)

            def per_feature(a, f=D):
                return a.unsqueeze(2).to_broadcast([P, C, f])

            K1 = 2
            with dve.Fori(0, NC) as c:
                step, n = steps(dve, node1.step, c * K1)
                inv = inv_deg[:, bass.ds(c * C, C)]
                dve.wait_ge(node1.turned, c + 2)
                step(nc.vector.tensor_scalar(col[:, 0, :], turned[:, :, D], 1.0, None, ALU.max))
                step(nc.vector.reciprocal(inv, col[:, 0, :]))
                nc.vector.tensor_tensor(neigh_nm[:, bass.ds(c * C, C), :], turned[:, :, 0:D], per_feature(inv),
                                        ALU.mult).then_inc(node1.copied, 1)
                assert n[0] == K1

            dve.wait_ge(s_weights, 160)
            nc.vector.tensor_scalar(half_b_gate2[:, :], b_gate2_sb[:, :], 0.5, None, ALU.mult).then_inc(s_half_bias, 1)
            nc.vector.memset(acc_a[:, :], 0.0)
            mean_pass(pass2, acc_b)

            def norm(node, step, src_ap, out_ap, scratch, stds, last_inc):
                mean, var, den, rstd = (col[:, q, :] for q in range(4))
                step(nc.vector.tensor_reduce(mean, src_ap, AX_X, ALU.add))
                step(nc.vector.tensor_scalar(mean, mean, 1.0 / D, None, ALU.mult))
                step(nc.vector.tensor_tensor(out_ap, src_ap, per_feature(mean), ALU.subtract))
                step(nc.vector.tensor_tensor(scratch, out_ap, out_ap, ALU.mult))
                step(nc.vector.tensor_reduce(var, scratch, AX_X, ALU.add))
                nc.vector.tensor_scalar(den, var, 1.0 / D, EPS, ALU.mult, ALU.add).then_inc(node.var, 1)
                dve.wait_ge(node.std, stds)
                step(nc.vector.reciprocal(rstd, den))
                last = nc.vector.tensor_tensor(out_ap, out_ap, per_feature(rstd), ALU.mult)
                last.then_inc(last_inc, 1) if last_inc is not None else step(last)

            K2 = 9
            dve.wait_ge(s_x, 16)
            dve.wait_ge(node1.copied, NC + 1)
            with dve.Fori(0, NC) as c:
                step, n = steps(dve, node2.step, c * K2)
                tiles = bass.ds(c * C, C)
                dve.wait_ge(node2.turned, c + 2)
                step(nc.vector.tensor_tensor(t0[:, :, :], turned[:, :, 0:D], per_feature(inv_deg[:, tiles]), ALU.mult))
                step(nc.vector.tensor_tensor(t1[:, :, :], t0[:, :, :], neigh_nm[:, tiles, :], ALU.add))
                step(nc.vector.scalar_tensor_tensor(out=t0[:, :, :], in0=t1[:, :, :], scalar=0.5,
                                                    in1=x_nm[:, tiles, :], op0=ALU.mult, op1=ALU.add))
                dve.wait_ge(node2.x_turned, c + 1)
                norm(node2, step, t0[:, :, :], t2[:, :, :], t1[:, :, :], c + 1, node2.normed)
                dve.wait_ge(node2.normed, c + 2)
                nc.vector.tensor_scalar(x_nm[:, tiles, :], t2[:, :, :], 0.0, None, ALU.add).then_inc(node2.hidden, 1)
                assert n[0] == K2, n

            for register in (more, wides):
                dve.reg_mov(register, 0)

            def add_node_part(g, k, i):
                dve.wait_ge(pass3.gathered[k], 16 * GT * (i + 1))
                for h in range(2):
                    dve.wait_ge(pre_summed, 2 * g + h + 1)
                    part = hid[:, k, HALF * h:HALF * h + HALF, 0:D2]
                    nc.vector.tensor_tensor(part, part, pre_ps[h], ALU.add).then_inc(pre_added, 1)

            def gate_products(g, k):
                dve.wait_ge(hidden_done, 2 * g + 2)
                nc.vector.tensor_tensor(prod[:, :, :], hid[:, k, :, 0:D],
                                        w_gate2_sb[:, :].unsqueeze(1).to_broadcast([P, GT, D]), ALU.mult)\
                    .then_inc(gate_prod, 1)
                dve.wait_ge(gate_prod, g + 1)
                nc.vector.tensor_reduce(gate_dot[:, :], prod[:, :, :], AX_X, ALU.add).then_inc(gate_dotted, 1)
                match(pass3, g)

            def weigh(g):
                dve.wait_ge(gate_tanhed, g + 1)
                nc.vector.tensor_scalar(gate[:, :], gate_tanh[:, :], 0.5, 0.5, ALU.mult, ALU.add).then_inc(gate_set, 1)
                dve.wait_ge(pass3.matched, g + 1)
                dve.wait_ge(gate_set, g + 1)
                nc.vector.tensor_tensor(hot[:, :, :], hot01[:, :, :], over_window(gate[:, :]), ALU.mult)\
                    .then_inc(pass3.hot_set, 1)

            add_node_part(0, 0, 0)
            add_node_part(1, 1, 0)
            gate_products(0, 0)
            weigh(0)

            def group(g, k, i):
                last = g if isinstance(g, int) else 0
                if last < NG - 2:
                    add_node_part(g + 2, (k + 2) % RING, i + (k + 2) // RING)
                if last < NG - 1:
                    gate_products(g + 1, (k + 1) % RING)
                add_windows(pass3, acc_a, g, k)
                if last < NG - 1:
                    weigh(g + 1)
            over_groups(dve, group)
            end_pass(pass3)

            K3 = 16
            dve.wait_ge(node2.hidden, NC)
            with dve.Fori(0, NC) as c:
                step, n = steps(dve, node3.step, c * K3)
                tiles = bass.ds(c * C, C)
                dve.wait_ge(node3.product, c + 2)
                nc.vector.tensor_tensor(t0[:, :, :], slots[:, 16:16 + C, 0:D], x_nm[:, tiles, :], ALU.add)\
                    .then_inc(node3.copied, 1)
                dve.wait_ge(node3.copied, c + 2)
                norm(node3, step, t0[:, :, :], t2[:, :, :], t1[:, :, :], 2 * c + 1, None)
                gain, shift = (ln_gb_sb[:, q * D:q * D + D].unsqueeze(1).to_broadcast([P, C, D]) for q in range(2))
                step(nc.vector.tensor_tensor(t0[:, :, :], t2[:, :, :], gain, ALU.mult))
                step(nc.vector.tensor_tensor(t1[:, :, :], t0[:, :, :], shift, ALU.add))
                step(nc.vector.tensor_tensor(t0[:, :, :], t1[:, :, :], x_nm[:, tiles, :], ALU.add))
                norm(node3, step, t0[:, :, :], out_nm[:, tiles, :], t1[:, :, :], 2 * c + 2, node3.normed)
                assert n[0] == K3, n


def kernel(x, src, dst, edge_attr_32, L1_gnn_mW1, L1_gnn_mb1, L1_gnn_mW2, L1_gnn_mb2, L1_gnn_gW1, L1_gnn_gb1,
           L1_gnn_gW2, L1_gnn_gb2, L1_gnn_uW1, L1_gnn_ub1, L1_gnn_uW2, L1_gnn_ub2, L1_gnn_ln_g, L1_gnn_ln_b):
    import numpy as np
    import concourse.bacc as bacc
    from concourse.bass_utils import run_bass_kernel_spmd

    (x, src, dst, ea, mW1, mb1, mW2, mb2, gW1, gb1, gW2, gb2, uW1, ub1, uW2, ub2, ln_g, ln_b) = (
        np.asarray(a) for a in (
            x, src, dst, edge_attr_32, L1_gnn_mW1, L1_gnn_mb1, L1_gnn_mW2, L1_gnn_mb2, L1_gnn_gW1, L1_gnn_gb1,
            L1_gnn_gW2, L1_gnn_gb2, L1_gnn_uW1, L1_gnn_ub1, L1_gnn_uW2, L1_gnn_ub2, L1_gnn_ln_g, L1_gnn_ln_b))
    pad = NG * GE - E

    def rows_of(*parts):
        return np.concatenate([p.reshape(-1, p.shape[-1]) for p in parts], axis=0)

    src_l = np.concatenate([src, np.zeros(pad, src.dtype)]).reshape(NG, GT, P)
    dst_l = np.concatenate([dst, np.full(pad, N, dst.dtype)]).reshape(NG, GT, P)
    ea_l = np.concatenate([ea, np.zeros((pad, DE), ea.dtype)]).reshape(NG, 2, HALF, P, DE)
    node_w = np.concatenate([rows_of(gW1[:D], gb1), rows_of(mW1[:D], mb1)], axis=1)
    edge_w = np.concatenate([gW1[D:], mW1[D:]], axis=1)
    edge_w_apart = np.zeros((HALF, DE, HALF, D2), edge_w.dtype)
    for t in range(HALF):
        edge_w_apart[t, :, t] = edge_w
    ins = {
        "x": np.concatenate([x, np.zeros((NP - N, D), x.dtype)]).reshape(P, NT * D),
        "src": src_l.transpose(0, 2, 1),
        "dst": dst_l.transpose(2, 0, 1).reshape(P, NG * GT),
        "ea": ea_l.transpose(0, 2, 4, 1, 3).reshape(NG, P, 2 * P),
        "w_node": node_w,
        "w_edge": edge_w_apart.reshape(P, HALF * D2),
        "w_msg2": rows_of(mW2, mb2),
        "w_gate2": np.tile(gW2.reshape(1, D), (P, 1)),
        "b_gate2": np.tile(gb2.reshape(1, 1), (P, 1)),
        "w_upd1x": uW1[:D],
        "w_upd1a": uW1[D:],
        "b_upd1": ub1.reshape(D, 1),
        "w_upd2": rows_of(uW2, ub2),
        "ln_gb": np.tile(np.concatenate([ln_g, ln_b]).reshape(1, 2 * D), (P, 1)),
    }
    nc = bacc.Bacc("TRN2", target_bir_lowering=False, num_devices=1)
    arrays, args = {}, []
    for name, a in ins.items():
        a = np.ascontiguousarray(a)
        arrays[f"in_{name}"] = a
        args.append(nc.dram_tensor(f"in_{name}", a.shape, mybir.dt.from_np(a.dtype), kind="ExternalInput").ap())
    args.append(nc.dram_tensor("out_nodes", (P, NT * D), F32, kind="ExternalOutput").ap())
    bass_gnn(nc, *args)
    r = run_bass_kernel_spmd(nc, [arrays], core_ids=[0])
    return r.results[0]["out_nodes"].reshape(NP, D)[:N]
```

```python
from contextlib import ExitStack

import concourse.bass as bass
from concourse import mybir

ALU = mybir.AluOpType
ACT = mybir.ActivationFunctionType
F32 = mybir.dt.float32
I32 = mybir.dt.int32
U32 = mybir.dt.uint32
AX_X = mybir.AxisListType.X

P = 128
N, E, D, DE = 6250, 206250, 96, 32
NT = -(-N // P)
NP = NT * P
GT = 8
GE = GT * P
NG = -(-E // GE)
RING = 4
ROUNDS = NG // RING
W = 64
NW = -(-(N + 1) // W)
AW = NP + W
DA = D + 1
D2 = 2 * D
C = 7
NC = NT // C
CN = C * P
HALF = GT // 2
LT = -(-(E - (NG - 1) * GE) // P)
EPS = 1e-5

assert NC * C == NT and (NG * GE - E) < GE and NW * W <= AW


def bass_gnn(nc, x, src, dst, ea, w_node, w_edge, w_msg2, w_gate2, b_gate2, w_upd1x, w_upd1a, b_upd1,
             w_upd2, ln_gb, out):
    neigh_table = nc.dram_tensor("neigh_table", [NP, D], F32, kind="Internal").ap()
    hidden_table = nc.dram_tensor("hidden_table", [NP, D2], F32, kind="Internal").ap()
    x_table = x.rearrange("p (t f) -> (p t) f", f=D)

    with ExitStack() as ctx:
        def sb(name, shape, dt=F32):
            return ctx.enter_context(nc.sbuf_tensor(name, shape, dt))

        def sem(name):
            return ctx.enter_context(nc.semaphore(name))

        ident = sb("ident", [P, P])
        iota_i = sb("iota_i", [P, W], I32)
        iota = sb("iota", [P, W])
        ones = sb("ones", [P, P])
        w_node_sb = sb("w_node_sb", [DA, D2])
        w_edge_sb = sb("w_edge_sb", [P, HALF, D2])
        w_msg2_sb = sb("w_msg2_sb", [DA, D])
        w_gate2_sb = sb("w_gate2_sb", [P, D])
        b_gate2_sb = sb("b_gate2_sb", [P, 1])
        half_b_gate2 = sb("half_b_gate2", [P, 1])
        w_upd1x_sb = sb("w_upd1x_sb", [D, D])
        w_upd1a_sb = sb("w_upd1a_sb", [D, D])
        b_upd1_sb = sb("b_upd1_sb", [D, 1])
        w_upd2_sb = sb("w_upd2_sb", [DA, D])
        ln_gb_sb = sb("ln_gb_sb", [P, 2 * D])

        local = sb("local", [P, NG, GT])
        ext = sb("ext", [P, 2, NG])
        ext_red = sb("ext_red", [P, 4])
        spread = sb("spread", [P, NG])
        wide = sb("wide", [P, NG])
        first = sb("first", [P, NG])
        n_win = sb("n_win", [P, NG])
        first_i = sb("first_i", [1, NG], I32)
        n_win_i = sb("n_win_i", [1, NG], I32)

        idx = sb("idx", [P, RING, GT], I32)
        rows = sb("rows", [P, RING, GT, DA])
        hid = sb("hid", [P, RING, GT, D2 + 1])
        ea_sb = sb("ea_sb", [P, RING, 2 * P])
        here = sb("here", [P, GT])
        hot = sb("hot", [P, GT, W])
        hot01 = sb("hot01", [P, GT, W])
        prod = sb("prod", [P, GT, D])
        ext_diag = prod[:, :, :].rearrange("p t f -> p (t f)")[:, 0:4 * P].rearrange("p (q n) -> p q n", q=4)
        gate_dot = sb("gate_dot", [P, GT])
        gate_tanh = sb("gate_tanh", [P, GT])
        gate = sb("gate", [P, GT])
        acc_a = sb("acc_a", [DA, AW])
        acc_b_all = sb("acc_b", [P, AW])
        acc_b = acc_b_all[0:DA, :]
        x_shift = acc_b_all[:, 0:NT * D].rearrange("p (t f) -> p t f", f=D)

        x_nm = sb("x_nm", [P, NT, D])
        neigh_nm = sb("neigh_nm", [P, NT, D])
        dst_i = neigh_nm[:, :, :].rearrange("p t f -> p (t f)")[:, 0:NG * GT].bitcast(I32)
        inv_deg = sb("inv_deg", [P, NT])
        xT = sb("xT", [D, NC, CN])
        stage = sb("stage", [DA, C, P])
        stage_x = sb("stage_x", [DA, C, P])
        aggT = sb("aggT", [D, CN])
        updT = sb("updT", [DA, CN])
        updated = sb("updated", [P, C, D])
        hop2 = sb("hop2", [P, C, D])
        normed_nm = sb("normed_nm", [P, C, D])
        bn = sb("bn", [P, 2, C, 6])
        mean_var = sb("mean_var", [P, 2, C, 2])
        var_eps = sb("var_eps", [P, 2, C])
        rstd = sb("rstd", [P, 2, C])
        deg = sb("deg", [P, C])
        minus_half = sb("minus_half", [P, C])
        hid_nm = sb("hid_nm", [P, C, D2])
        out_nm = neigh_nm

        psum = ctx.enter_context(nc.psum_tensor("psum", [P, 8, 512], F32))
        win_ps = psum[0:DA, 0, 0:W]
        pre_ps = [psum[:, 1 + 2 * h:3 + 2 * h, :].rearrange("p b (t n) -> p (b t) n", t=2)[:, :, 0:D2]
                  for h in range(2)]
        slots = psum[:, :, :].rearrange("p b (s n) -> p (b s) n", n=P)
        turned = slots[:, 0:C, :]
        turned_x = slots[:, 8:8 + C, :]
        hid_ps = psum[:, 4:8, :].rearrange("p b (t n) -> p (b t) n", t=2)[:, 0:C, 0:D2]

        s_weights = sem("s_weights")
        s_dst = sem("s_dst")
        s_x = sem("s_x")
        s_pool_const = sem("s_pool_const")
        s_pro = sem("s_pro")
        s_ext_turned = sem("s_ext_turned")
        s_ext_spread = sem("s_ext_spread")
        s_meta = sem("s_meta")
        s_ones = sem("s_ones")
        s_half_bias = sem("s_half_bias")
        s_half = sem("s_half")

        class EdgePass:
            def __init__(self, name):
                self.idx_loaded = [sem(f"{name}_idx_loaded{k}") for k in range(RING)]
                self.gathered = [sem(f"{name}_gathered{k}") for k in range(RING)]
                self.row_free = [sem(f"{name}_row_free{k}") for k in range(RING)]
                self.matched = sem(f"{name}_matched")
                self.hot_set = sem(f"{name}_hot_set")
                self.window_summed = sem(f"{name}_window_summed")
                self.window_added = sem(f"{name}_window_added")
                self.here_set = sem(f"{name}_here_set")
                self.here_moved = sem(f"{name}_here_moved")
                self.more_matched = sem(f"{name}_more_matched")
                self.more_hot_set = sem(f"{name}_more_hot_set")
                self.more_summed = sem(f"{name}_more_summed")
                self.more_added = sem(f"{name}_more_added")
                self.done = sem(f"{name}_done")

        pass1, pass2, pass3 = EdgePass("p1"), EdgePass("p2"), EdgePass("p3")
        ea_loaded = [sem(f"ea_loaded{k}") for k in range(RING)]
        pre_summed = sem("pre_summed")
        pre_added = sem("pre_added")
        hidden_done = sem("hidden_done")
        gate_prod = sem("gate_prod")
        gate_dotted = sem("gate_dotted")
        gate_tanhed = sem("gate_tanhed")
        gate_set = sem("gate_set")

        class NodePhase:
            def __init__(self, name):
                self.staged = sem(f"{name}_staged")
                self.turned = sem(f"{name}_turned")
                self.step = sem(f"{name}_step")
                self.read = sem(f"{name}_read")
                self.var = [sem(f"{name}_var{q}") for q in range(2)]
                self.rstd = [sem(f"{name}_rstd{q}") for q in range(2)]
                self.normed = sem(f"{name}_normed")
                self.affine = sem(f"{name}_affine")
                self.x_kept = sem(f"{name}_x_kept")
                self.x_turned = sem(f"{name}_x_turned")
                self.x_staged = sem(f"{name}_x_staged")
                self.product = sem(f"{name}_product")
                self.copied = sem(f"{name}_copied")
                self.hidden = sem(f"{name}_hidden")
                self.out_done = sem(f"{name}_out_done")
                self.stored = sem(f"{name}_stored")

        node1, node2, node3 = NodePhase("n1"), NodePhase("n2"), NodePhase("n3")

        block = ctx.enter_context(nc.Block())

        def steps(eng, sem_, base):
            n = [0]

            def step(ins):
                n[0] += 1
                ins.then_inc(sem_, 1)
                eng.wait_ge(sem_, base + n[0])
            return step, n

        def tiles_of(g):
            return LT if isinstance(g, int) and g == NG - 1 else GT

        def gathered_by(g, i):
            return 16 * (GT * i + tiles_of(g))

        def last_turn(k):
            return range(k, NG, RING)[-1], len(range(k, NG, RING)) - 1

        def over_groups(eng, body, last=NG, peeled=0):
            turns = last // RING - peeled
            with eng.Fori(0, turns) as i:
                for k in range(RING):
                    body(i * RING + k, k, i)
            for g in range(turns * RING, last):
                body(g, g % RING, g // RING)

        @block.sync
        def _(sp):
            def load_idx(ps, g, k):
                sp.dma_start(idx[:, k, :], src[bass.ds(g, 1), :, :].rearrange("g p t -> (g p) t")).then_inc(
                    ps.idx_loaded[k], 16)

            def load_ea(g, k):
                sp.dma_start(ea_sb[:, k, :], ea[bass.ds(g, 1), :, :].rearrange("g p n -> (g p) n")).then_inc(
                    ea_loaded[k], 16)

            for k in range(RING):
                load_idx(pass1, k, k)
            sp.dma_start(dst_i, dst).then_inc(s_dst, 16)
            for to, of in ((w_node_sb[:, :], w_node), (w_edge_sb[:, :, :].rearrange("p t n -> p (t n)"), w_edge),
                           (w_msg2_sb[:, :], w_msg2), (w_gate2_sb[:, :], w_gate2),
                           (b_gate2_sb[:, :], b_gate2), (w_upd1x_sb[:, :], w_upd1x), (w_upd1a_sb[:, :], w_upd1a),
                           (b_upd1_sb[:, :], b_upd1), (w_upd2_sb[:, :], w_upd2), (ln_gb_sb[:, :], ln_gb)):
                sp.dma_start(to, of).then_inc(s_weights, 16)
            sp.dma_start(x_nm[:, :, :].rearrange("p t f -> p (t f)"), x).then_inc(s_x, 16)

            def feed(ps):
                def refill(g, k, i):
                    sp.wait_ge(ps.gathered[k], 16 * GT * (i + 1))
                    load_idx(ps, g + RING, k)
                over_groups(sp, refill, NG - RING)

            def store_table(node, table, of, f):
                view = table.rearrange("(p t) f -> p (t f)", p=P)
                with sp.Fori(0, NC) as c:
                    sp.wait_ge(node.copied, c + 2)
                    sp.dma_start(view[:, bass.ds(c * (C * f), C * f)], of(c)).then_inc(node.stored, 16)

            feed(pass1)
            for k in range(RING):
                sp.wait_ge(pass1.gathered[k], gathered_by(*last_turn(k)))
                load_idx(pass2, k, k)
            flat = neigh_nm[:, :, :].rearrange("p t f -> p (t f)")
            store_table(node1, neigh_table, lambda c: flat[:, bass.ds(c * (C * D), C * D)], D)
            feed(pass2)
            for k in range(RING):
                sp.wait_ge(pass2.gathered[k], gathered_by(*last_turn(k)))
                load_idx(pass3, k, k)
                load_ea(k, k)
            with sp.Fori(0, NC) as c:
                sp.wait_ge(node2.copied, c + 2)
                sp.dma_start(hidden_table.rearrange("(p t) f -> p (t f)", p=P)[:, bass.ds(c * (C * D2), C * D2)],
                             hid_nm[:, :, :].rearrange("p t f -> p (t f)")).then_inc(node2.stored, 16)

            def refill3(g, k, i):
                sp.wait_ge(pass3.gathered[k], 16 * GT * (i + 1))
                load_idx(pass3, g + RING, k)
                sp.wait_ge(pre_summed, 2 * g + 2)
                load_ea(g + RING, k)
            over_groups(sp, refill3, NG - RING)

            with sp.Fori(0, NC) as c:
                sp.wait_ge(node3.out_done, c + 1)
                sp.dma_start(out[:, bass.ds(c * (C * D), C * D)],
                             out_nm[:, :, :].rearrange("p t f -> p (t f)")[:, bass.ds(c * (C * D), C * D)]).then_inc(
                    node3.stored, 16)
            sp.wait_ge(node3.stored, 16 * NC)

        @block.gpsimd
        def _(pool):
            nc.gpsimd.memset(ident[:], 0.0).then_inc(s_pool_const, 1)
            nc.gpsimd.iota(iota_i[:], pattern=[[1, W]], base=0, channel_multiplier=0).then_inc(s_pool_const, 1)
            pool.wait_ge(s_pool_const, 2)
            nc.gpsimd.affine_select(out=ident[:], in_=ident[:], compare_op=ALU.not_equal, fill=1.0, base=0,
                                    pattern=[[-1, P]], channel_multiplier=1).then_inc(s_pool_const, 1)

            def gather_all(ps, table, buf, width):
                def gather(g, k, i):
                    pool.wait_ge(ps.idx_loaded[k], 16 * (i + 1))
                    pool.wait_ge(ps.row_free[k], i + 1)
                    pool.nop(nofuse=True)
                    for t in range(tiles_of(g)):
                        pool.indirect_dma_start(
                            buf[:, k, t, 0:width], None, table,
                            bass.IndirectOffsetOnAxis(ap=idx[:, k, t:t + 1].bitcast(U32), axis=0),
                        ).then_inc(ps.gathered[k], 16)
                over_groups(pool, gather)

            gather_all(pass1, x_table, rows, D)
            pool.wait_ge(node1.stored, 16 * NC)
            gather_all(pass2, neigh_table, rows, D)

            def power(node, q, c):
                pool.wait_ge(node.var[q], c + 1)
                nc.gpsimd.tensor_tensor(rstd[:, q, :], var_eps[:, q, :], minus_half[:, :], ALU.pow)\
                    .then_inc(node.rstd[q], 1)

            with pool.Fori(0, NC) as c:
                power(node2, 0, c)
            pool.wait_ge(node2.stored, 16 * (NC + 1))
            gather_all(pass3, hidden_table, hid, D2)

            def affine(c):
                part = out_nm[:, bass.ds(c * C, C), :]
                gain = ln_gb_sb[:, 0:D].unsqueeze(1).to_broadcast([P, C, D])
                pool.wait_ge(node3.normed, c + 1)
                for n, (other, op) in enumerate(((gain, ALU.mult), (x_shift[:, bass.ds(c * C, C), :], ALU.add))):
                    if n:
                        pool.wait_ge(node3.affine, 2 * c + n)
                    pool.nop(nofuse=True)
                    nc.gpsimd.tensor_tensor(part, part, other, op).then_inc(node3.affine, 1)

            pool.wait_ge(s_half, 3)
            power(node3, 0, 0)
            affine(0)
            with pool.Fori(0, NC - 1) as c:
                power(node3, 0, c + 1)
                power(node3, 1, c)
                affine(c + 1)
            power(node3, 1, NC - 1)

        @block.tensor
        def _(pe):
            more = pe.alloc_register("pe_more_windows")

            def sum_windows(ps, g, k, i, rhs_rows):
                n = pe.value_load(n_win_i[0:1, bass.ds(g, 1)], min_val=1, max_val=NW)
                pe.wait_ge(ps.gathered[k], gathered_by(g, i))
                if ps is pass3:
                    pe.wait_ge(hidden_done, 2 * g + 2)
                pe.wait_ge(ps.hot_set, g + 1)
                for t in range(tiles_of(g)):
                    mm = nc.tensor.matmul(win_ps, rhs_rows(k, t), hot[:, t, :], start=(t == 0),
                                          stop=(t == tiles_of(g) - 1))
                mm.then_inc(ps.window_summed, 1)
                with pe.If(n > 1):
                    with pe.Fori(1, n):
                        pe.wait_ge(ps.more_hot_set, pe.snap(more, min_val=0, max_val=NG * NW) + 1)
                        for t in range(tiles_of(g)):
                            mm = nc.tensor.matmul(win_ps, rhs_rows(k, t), hot[:, t, :], start=(t == 0),
                                                  stop=(t == tiles_of(g) - 1))
                        mm.then_inc(ps.more_summed, 1)
                        pe.reg_add(more, more, 1)

            pe.wait_ge(s_pool_const, 3)
            pe.wait_ge(s_pro, 2)
            halves = [(0, P), (P, NG)]
            for q in range(4):
                a, b = halves[q % 2]
                mm = nc.tensor.transpose(psum[0:b - a, 1 + q, 0:P], ext[:, q // 2, a:b], ident[:, :])
            mm.then_inc(s_ext_turned, 1)
            pe.wait_ge(s_pro, 4)
            for q in range(4):
                a, b = halves[q % 2]
                mm = nc.tensor.matmul(psum[:, 5 + q // 2, a:b], ones[0:b - a, :], ext_diag[0:b - a, q, 0:b - a],
                                      start=True, stop=True)
            mm.then_inc(s_ext_spread, 1)

            pe.wait_ge(s_meta, 1)
            pe.reg_mov(more, 0)
            over_groups(pe, lambda g, k, i: sum_windows(pass1, g, k, i, lambda k, t: rows[:, k, t, :]))

            with pe.Fori(0, NC) as c:
                pe.wait_ge(node1.staged, c + 1)
                pe.wait_ge(node1.copied, c + 1)
                for j in range(C):
                    mm = nc.tensor.transpose(turned[:, j, 0:DA], stage[:, j, :], ident[0:DA, 0:DA])
                mm.then_inc(node1.turned, 1)

            pe.wait_ge(node1.copied, NC + 1)
            pe.reg_mov(more, 0)
            over_groups(pe, lambda g, k, i: sum_windows(pass2, g, k, i, lambda k, t: rows[:, k, t, :]))

            pe.wait_ge(s_weights, 160)

            def turn_sums(c):
                pe.wait_ge(node2.staged, c + 1)
                pe.wait_ge(node2.read, c + 1)
                for j in range(C):
                    mm = nc.tensor.transpose(turned[:, j, 0:DA], stage[:, j, :], ident[0:DA, 0:DA])
                mm.then_inc(node2.turned, 1)

            def turn_x(c):
                pe.wait_ge(node2.normed, c + 1)
                pe.wait_ge(node2.x_kept, c + 1)
                for j in range(C):
                    mm = nc.tensor.transpose(turned_x[0:D, j, :], normed_nm[:, j, :], ident[:, :])
                mm.then_inc(node2.x_turned, 1)

            def hidden_chunk(c):
                pe.wait_ge(node2.x_staged, c + 1)
                pe.wait_ge(node2.copied, c + 1)
                for j in range(C):
                    mm = nc.tensor.matmul(hid_ps[:, j, :], stage_x[:, j, :], w_node_sb[:, :], start=True, stop=True)
                mm.then_inc(node2.product, 1)

            turn_sums(0)
            turn_sums(1)
            with pe.Fori(0, NC - 2) as c:
                turn_x(c)
                turn_sums(c + 2)
                hidden_chunk(c)
            for c in range(NC - 2, NC):
                turn_x(c)
                hidden_chunk(c)

            def edge_part(g, k, i, free):
                pe.wait_ge(ea_loaded[k], 16 * (i + 1))
                for h in range(2):
                    if free:
                        pe.wait_ge(pre_added, 2 * g + h - 1)
                    for t in range(HALF):
                        mm = nc.tensor.matmul(pre_ps[h][:, t, :],
                                              ea_sb[:, k, h * P:h * P + P], w_edge_sb[:, t, :], start=True, stop=True)
                    mm.then_inc(pre_summed, 1)

            pe.wait_ge(node2.copied, NC + 1)
            pe.reg_mov(more, 0)
            edge_part(0, 0, 0, False)
            edge_part(1, 1, 0, True)

            def edge_group(g, k, i):
                if not (isinstance(g, int) and g >= NG - 2):
                    edge_part(g + 2, (k + 2) % RING, i + (k + 2) // RING, True)
                sum_windows(pass3, g, k, i, lambda k, t: hid[:, k, t, D:D2 + 1])
            over_groups(pe, edge_group)

            flat_stage = stage[:, :, :].rearrange("f c n -> f (c n)")
            flat_xT = xT[:, :, :].rearrange("f c n -> f (c n)")

            def second_message_layer(c):
                pe.wait_ge(node3.staged, c + 1)
                for q in range(2):
                    mm = nc.tensor.matmul(psum[0:D, q, 0:CN // 2], w_msg2_sb[:, :],
                                          flat_stage[:, q * (CN // 2):(q + 1) * (CN // 2)], start=True, stop=True)
                mm.then_inc(node3.turned, 1)

            def first_update_layer(c):
                for q in range(2):
                    nc.tensor.matmul(psum[0:D, 2 + q, 0:CN // 2], w_upd1x_sb[:, :],
                                     flat_xT[:, bass.ds(c * CN + q * (CN // 2), CN // 2)], start=True, stop=False)
                pe.wait_ge(node3.x_staged, c + 1)
                for q in range(2):
                    mm = nc.tensor.matmul(psum[0:D, 2 + q, 0:CN // 2], w_upd1a_sb[:, :],
                                          aggT[:, q * (CN // 2):(q + 1) * (CN // 2)], start=False, stop=True)
                mm.then_inc(node3.x_turned, 1)

            def second_update_layer(c):
                pe.wait_ge(node3.hidden, c + 1)
                pe.wait_ge(node3.copied, c + 1)
                for j in range(C):
                    mm = nc.tensor.matmul(slots[:, 16 + j, 0:D], updT[:, j * P:(j + 1) * P], w_upd2_sb[:, :],
                                          start=True, stop=True)
                mm.then_inc(node3.product, 1)

            second_message_layer(0)
            with pe.Fori(0, NC - 1) as c:
                first_update_layer(c)
                second_message_layer(c + 1)
                second_update_layer(c)
            first_update_layer(NC - 1)
            second_update_layer(NC - 1)

        @block.scalar
        def _(act):
            def stage_acc(acc, c):
                view = acc[:, 0:NP].rearrange("f (p t) -> f t p", t=NT)
                return nc.scalar.copy(stage[:, :, :], view[:, bass.ds(c * C, C), :])

            act.wait_ge(pass1.done, 1)
            with act.Fori(0, NC) as c:
                act.wait_ge(node1.turned, c + 1)
                stage_acc(acc_a, c).then_inc(node1.staged, 1)

            act.wait_ge(pass2.done, 1)
            act.wait_ge(node1.turned, NC + 1)

            def copy_hidden(c):
                act.wait_ge(node2.x_turned, c + 2)
                nc.scalar.copy(stage_x[0:D, :, :], turned_x[0:D, :, :]).then_inc(node2.x_staged, 1)
                nc.scalar.copy(xT[:, bass.ds(c, 1), :].rearrange("f a n -> f (a n)"),
                               psum[0:D, 2:4, :].rearrange("p b n -> p (b n)")[:, 0:CN]).then_inc(node2.x_kept, 1)
                act.wait_ge(node2.product, c + 1)
                act.wait_ge(node2.stored, 16 * c + 16)
                nc.scalar.copy(hid_nm[:, :, :], hid_ps).then_inc(node2.copied, 1)

            def stage_sums(c):
                act.wait_ge(node2.turned, c + 1)
                stage_acc(acc_b, c).then_inc(node2.staged, 1)

            stage_sums(0)
            stage_sums(1)
            with act.Fori(0, NC - 2) as c:
                stage_sums(c + 2)
                copy_hidden(c)
            for c in range(NC - 2, NC):
                copy_hidden(c)

            def gelu(g, k):
                for h in range(2):
                    act.wait_ge(pre_added, 2 * g + h + 1)
                    part = hid[:, k, HALF * h:HALF * h + HALF, 0:D2]
                    nc.scalar.activation(part, part, ACT.Gelu).then_inc(hidden_done, 1)

            def tanh(g):
                act.wait_ge(gate_dotted, g + 1)
                nc.scalar.activation(gate_tanh[:, :], gate_dot[:, :], ACT.Tanh, bias=half_b_gate2[:, 0:1],
                                     scale=0.5).then_inc(gate_tanhed, 1)

            act.wait_ge(s_half_bias, 1)
            gelu(0, 0)
            gelu(1, 1)
            tanh(0)

            def group(g, k, i):
                last = g if isinstance(g, int) else 0
                if last < NG - 2:
                    gelu(g + 2, (k + 2) % RING)
                if last < NG - 1:
                    tanh(g + 1)
            over_groups(act, group)

            act.wait_ge(pass3.done, 1)

            def copy_aggregate(c):
                act.wait_ge(node3.turned, c + 2)
                nc.scalar.copy(aggT[:, :].rearrange("f (q n) -> f q n", q=2),
                               psum[0:D, 0:2, 0:CN // 2]).then_inc(node3.x_staged, 1)

            def update_gelu(c):
                act.wait_ge(node3.x_turned, c + 1)
                act.wait_ge(node3.product, c + 1)
                nc.scalar.activation(updT[0:D, :].rearrange("f (q n) -> f q n", q=2), psum[0:D, 2:4, 0:CN // 2],
                                     ACT.Gelu, bias=b_upd1_sb[:, 0:1]).then_inc(node3.hidden, 1)

            stage_acc(acc_a, 0).then_inc(node3.staged, 1)
            with act.Fori(0, NC - 1) as c:
                copy_aggregate(c)
                stage_acc(acc_a, c + 1).then_inc(node3.staged, 1)
                update_gelu(c)
            copy_aggregate(NC - 1)
            update_gelu(NC - 1)

        @block.vector
        def _(dve):
            nc.vector.memset(minus_half[:, :], -0.5)
            for one in (ones[:, :], rows[:, :, :, D:DA], hid[:, :, :, D2:D2 + 1], stage_x[D:DA, :, :], updT[D:DA, :]):
                last = nc.vector.memset(one, 1.0)
            last.then_inc(s_ones, 1)
            dve.wait_ge(s_ones, 1)
            for ps in (pass1, pass2, pass3):
                for free in (*ps.row_free, ps.window_added, ps.more_added):
                    dve.sem_inc(free, 1)
            for free in (node1.turned, node1.copied, node2.turned, node2.read, node2.x_turned, node2.x_kept,
                         node2.copied, node3.turned, node3.product, node3.copied):
                dve.sem_inc(free, 1)
            dve.sem_inc(node2.stored, 16)

            step, n = steps(dve, s_pro, 0)
            dve.wait_ge(s_dst, 16)
            step(nc.vector.tensor_copy(local[:, :, :].rearrange("p g t -> p (g t)"), dst_i))
            nc.vector.tensor_reduce(ext[:, 0, :], local[:, :, :], AX_X, ALU.max)
            step(nc.vector.tensor_reduce(ext[:, 1, :], local[:, :, :], AX_X, ALU.min, negate=True))
            dve.wait_ge(s_ext_turned, 1)
            parts = [P, NG - P, P, NG - P]
            for q in range(4):
                last = nc.vector.tensor_reduce(ext_red[0:parts[q], q:q + 1], psum[0:parts[q], 1 + q, 0:P], AX_X,
                                               ALU.max)
            step(last)
            for q in range(4):
                last = nc.vector.tensor_scalar(ext_diag[0:parts[q], q, 0:parts[q]], ident[0:parts[q], 0:parts[q]],
                                               ext_red[0:parts[q], q:q + 1], None, ALU.mult)
            step(last)
            dve.wait_ge(s_ext_spread, 1)
            largest, neg_least = psum[:, 5, 0:NG], psum[:, 6, 0:NG]
            step(nc.vector.tensor_copy(first[:, :], neg_least))
            step(nc.vector.tensor_tensor(spread[:, :], largest, first[:, :], ALU.add))
            step(nc.vector.tensor_scalar(wide[:, :], spread[:, :], float(W), None, ALU.is_ge))
            step(nc.vector.tensor_scalar(n_win[:, :], wide[:, :], float(NW - 1), 1.0, ALU.mult, ALU.add))
            step(nc.vector.tensor_scalar(wide[:, :], wide[:, :], -1.0, None, ALU.add))
            step(nc.vector.tensor_tensor(first[:, :], first[:, :], wide[:, :], ALU.mult))
            step(nc.vector.tensor_tensor(local[:, :, :], local[:, :, :],
                                         first[:, :].unsqueeze(2).to_broadcast([P, NG, GT]), ALU.subtract))
            nc.vector.tensor_copy(first_i[:, :], first[0:1, :])
            step(nc.vector.tensor_copy(n_win_i[:, :], n_win[0:1, :]))
            dve.sem_inc(s_meta, 1)
            dve.wait_ge(s_pool_const, 3)
            nc.vector.tensor_copy(iota[:, :], iota_i[:, :])
            nc.vector.memset(acc_a[:, :], 0.0)
            step(nc.vector.memset(acc_b[:, :], 0.0))

            more = dve.alloc_register("dve_more_windows")
            wides = dve.alloc_register("dve_wide_groups")
            column = dve.alloc_register("dve_column")
            over_tiles = iota[:, :].unsqueeze(1).to_broadcast([P, GT, W])

            def over_window(a):
                return a.unsqueeze(2).to_broadcast([P, GT, W])

            def match(ps, g):
                to = hot01 if ps is pass3 else hot
                nc.vector.tensor_tensor(to[:, :, :], over_tiles,
                                        over_window(local[:, bass.ds(g, 1), :].rearrange("p g t -> p (g t)")),
                                        ALU.is_equal).then_inc(ps.matched if ps is pass3 else ps.hot_set, 1)

            def add_windows(ps, acc, g, k):
                n = dve.value_load(n_win_i[0:1, bass.ds(g, 1)], min_val=1, max_val=NW)
                base = dve.value_load(first_i[0:1, bass.ds(g, 1)], min_val=0, max_val=N)
                dve.wait_ge(ps.window_summed, g + 1)
                dve.wait_ge(ps.window_added, g + 1)
                cols = acc[:, bass.ds(base, W)]
                nc.vector.tensor_tensor(cols, cols, win_ps, ALU.add).then_inc(ps.window_added, 1)
                with dve.If(n > 1):
                    nc.vector.tensor_scalar(here[:, :], local[:, bass.ds(g, 1), :].rearrange("p g t -> p (g t)"),
                                            0.0, None, ALU.add).then_inc(ps.here_set, 1)
                    dve.reg_mov(column, W)
                    with dve.Fori(1, n):
                        before = dve.snap(more, min_val=0, max_val=NG * NW)
                        dve.wait_ge(ps.here_set, dve.snap(wides, min_val=0, max_val=NG) + 1)
                        dve.wait_ge(ps.more_added, before + 1)
                        nc.vector.tensor_scalar(here[:, :], here[:, :], -float(W), None, ALU.add)\
                            .then_inc(ps.here_moved, 1)
                        dve.wait_ge(ps.here_moved, before + 1)
                        nc.vector.tensor_tensor(hot[:, :, :], over_tiles, over_window(here[:, :]), ALU.is_equal)\
                            .then_inc(ps.more_matched, 1)
                        dve.wait_ge(ps.more_matched, before + 1)
                        factor = over_window(gate[:, :]) if ps is pass3 else hot[:, :, :]
                        nc.vector.tensor_tensor(hot[:, :, :], hot[:, :, :], factor, ALU.mult)\
                            .then_inc(ps.more_hot_set, 1)
                        dve.wait_ge(ps.more_summed, before + 1)
                        dve.wait_ge(ps.window_added, g + 2)
                        cols = acc[:, bass.ds(dve.snap(column, min_val=0, max_val=AW - W), W)]
                        nc.vector.tensor_tensor(cols, cols, win_ps, ALU.add).then_inc(ps.more_added, 1)
                        dve.reg_add(more, more, 1)
                        dve.reg_add(column, column, W)
                    dve.reg_add(wides, wides, 1)
                dve.sem_inc(ps.row_free[k], 1)

            def end_pass(ps):
                dve.wait_ge(ps.window_added, NG + 1)
                dve.wait_ge(ps.more_added, dve.snap(more, min_val=0, max_val=NG * NW) + 1)
                dve.sem_inc(ps.done, 1)

            def mean_pass(ps, acc):
                for register in (more, wides):
                    dve.reg_mov(register, 0)
                match(ps, 0)

                def group(g, k, i):
                    add_windows(ps, acc, g, k)
                    if not (isinstance(g, int) and g == NG - 1):
                        match(ps, g + 1)
                over_groups(dve, group)
                end_pass(ps)

            mean_pass(pass1, acc_a)

            def per_feature(a):
                return a.unsqueeze(2).to_broadcast([P, C, D])

            K1 = 2
            with dve.Fori(0, NC) as c:
                step, n = steps(dve, node1.step, c * K1)
                inv = inv_deg[:, bass.ds(c * C, C)]
                dve.wait_ge(node1.turned, c + 2)
                step(nc.vector.tensor_scalar(deg[:, :], turned[:, :, D], 1.0, None, ALU.max))
                step(nc.vector.reciprocal(inv, deg[:, :]))
                nc.vector.tensor_tensor(neigh_nm[:, bass.ds(c * C, C), :], turned[:, :, 0:D], per_feature(inv),
                                        ALU.mult).then_inc(node1.copied, 1)
                assert n[0] == K1

            dve.wait_ge(s_weights, 160)
            nc.vector.tensor_scalar(half_b_gate2[:, :], b_gate2_sb[:, :], 0.5, None, ALU.mult).then_inc(s_half_bias, 1)
            nc.vector.memset(acc_a[:, :], 0.0)
            dve.wait_ge(s_x, 16)
            dve.wait_ge(node1.copied, NC + 1)
            nc.vector.scalar_tensor_tensor(out=x_nm[:, :, :], in0=neigh_nm[:, :, :], scalar=0.5, in1=x_nm[:, :, :],
                                           op0=ALU.mult, op1=ALU.add).then_inc(s_half, 1)
            nc.vector.tensor_scalar(inv_deg[:, :], inv_deg[:, :], 0.5, None, ALU.mult).then_inc(s_half, 1)
            mean_pass(pass2, acc_b)
            dve.wait_ge(s_half, 2)

            def moments(node, q, step, chunk):
                dve.nop(nofuse=True)
                for j in range(C):
                    last = nc.vector.bn_stats(bn[:, q, j, :], chunk(j))
                step(last)
                dve.nop(nofuse=True)
                for j in range(C):
                    last = nc.vector.bn_aggr(mean_var[:, q, j, :], bn[:, q, j, :])
                step(last)
                nc.vector.tensor_scalar(var_eps[:, q, :], mean_var[:, q, :, 1], EPS, None, ALU.add)\
                    .then_inc(node.var[q], 1)

            def standardize(node, q, c, chunk, to, done):
                dve.wait_ge(node.rstd[q], c + 1)
                for j in range(C):
                    last = nc.vector.tensor_scalar(to(j), chunk(j), mean_var[:, q, j, 0:1], rstd[:, q, j:j + 1],
                                                   ALU.subtract, ALU.mult)
                last.then_inc(done, 1)

            def at(a, c):
                return lambda j: a[:, bass.ds(c * C + j, 1), :].rearrange("p t f -> p (t f)")

            def mix(c, before):
                step, n = steps(dve, node2.step, before)
                tiles = bass.ds(c * C, C)
                dve.wait_ge(node2.turned, c + 2)
                nc.vector.tensor_tensor(hop2[:, :, :], turned[:, :, 0:D], per_feature(inv_deg[:, tiles]), ALU.mult)\
                    .then_inc(node2.read, 1)
                dve.wait_ge(node2.read, c + 2)
                step(nc.vector.tensor_tensor(x_nm[:, tiles, :], hop2[:, :, :], x_nm[:, tiles, :], ALU.add))
                assert n[0] == 1

            def first_moments(c, before):
                step, n = steps(dve, node2.step, before)
                moments(node2, 0, step, at(x_nm, c))
                assert n[0] == 2

            def normed_x(c, before):
                step, n = steps(dve, node2.step, before)
                dve.wait_ge(node2.x_turned, c + 1)
                standardize(node2, 0, c, at(x_nm, c), lambda j: normed_nm[:, j, :], node2.normed)
                dve.wait_ge(node2.normed, c + 1)
                step(nc.vector.tensor_scalar(x_nm[:, bass.ds(c * C, C), :], normed_nm[:, :, :], 0.0, None, ALU.add))
                assert n[0] == 1

            K2 = 4
            mix(0, 0)
            with dve.Fori(0, NC - 1) as c:
                first_moments(c, K2 * c + 1)
                mix(c + 1, K2 * c + 3)
                normed_x(c, K2 * c + 4)
            first_moments(NC - 1, K2 * (NC - 1) + 1)
            normed_x(NC - 1, K2 * (NC - 1) + 3)

            dve.wait_ge(node2.step, K2 * NC)
            nc.vector.tensor_tensor(x_shift[:, :, :], x_nm[:, :, :],
                                    ln_gb_sb[:, D:2 * D].unsqueeze(1).to_broadcast([P, NT, D]), ALU.add)\
                .then_inc(s_half, 1)

            for register in (more, wides):
                dve.reg_mov(register, 0)

            def add_node_part(g, k, i):
                dve.wait_ge(pass3.gathered[k], gathered_by(g, i))
                for h in range(2):
                    dve.wait_ge(pre_summed, 2 * g + h + 1)
                    part = hid[:, k, HALF * h:HALF * h + HALF, 0:D2]
                    nc.vector.tensor_tensor(part, part, pre_ps[h], ALU.add).then_inc(pre_added, 1)

            def gate_products(g, k):
                dve.wait_ge(hidden_done, 2 * g + 2)
                nc.vector.tensor_tensor(prod[:, :, :], hid[:, k, :, 0:D],
                                        w_gate2_sb[:, :].unsqueeze(1).to_broadcast([P, GT, D]), ALU.mult)\
                    .then_inc(gate_prod, 1)
                dve.wait_ge(gate_prod, g + 1)
                nc.vector.tensor_reduce(gate_dot[:, :], prod[:, :, :], AX_X, ALU.add).then_inc(gate_dotted, 1)
                match(pass3, g)

            def weigh(g):
                dve.wait_ge(gate_tanhed, g + 1)
                nc.vector.tensor_scalar(gate[:, :], gate_tanh[:, :], 0.5, 0.5, ALU.mult, ALU.add).then_inc(gate_set, 1)
                dve.wait_ge(pass3.matched, g + 1)
                dve.wait_ge(gate_set, g + 1)
                nc.vector.tensor_tensor(hot[:, :, :], hot01[:, :, :], over_window(gate[:, :]), ALU.mult)\
                    .then_inc(pass3.hot_set, 1)

            add_node_part(0, 0, 0)
            add_node_part(1, 1, 0)
            gate_products(0, 0)
            weigh(0)

            def group(g, k, i):
                last = g if isinstance(g, int) else 0
                if last < NG - 2:
                    add_node_part(g + 2, (k + 2) % RING, i + (k + 2) // RING)
                if last < NG - 1:
                    gate_products(g + 1, (k + 1) % RING)
                add_windows(pass3, acc_a, g, k)
                if last < NG - 1:
                    weigh(g + 1)
            over_groups(dve, group, peeled=1)
            end_pass(pass3)

            def update(c, before, first=False):
                step, n = steps(dve, node3.step, before)
                dve.wait_ge(node3.product, c + 2)
                if not first:
                    dve.wait_ge(node3.normed, c)
                nc.vector.tensor_tensor(updated[:, :, :], slots[:, 16:16 + C, 0:D], x_nm[:, bass.ds(c * C, C), :],
                                        ALU.add).then_inc(node3.copied, 1)
                dve.wait_ge(node3.copied, c + 2)
                moments(node3, 0, step, lambda j: updated[:, j, :])
                assert n[0] == 2

            def first_norm(c):
                standardize(node3, 0, c, lambda j: updated[:, j, :], at(out_nm, c), node3.normed)

            def outer_moments(c, before, first=False):
                step, n = steps(dve, node3.step, before)
                dve.wait_ge(node3.affine, 2 * c + 2)
                if not first:
                    dve.wait_ge(node3.out_done, c)
                moments(node3, 1, step, at(out_nm, c))
                assert n[0] == 2

            def second_norm(c):
                standardize(node3, 1, c, at(out_nm, c), at(out_nm, c), node3.out_done)

            update(0, 0, first=True)
            first_norm(0)
            update(1, 2)
            outer_moments(0, 4, first=True)
            with dve.Fori(1, NC - 1) as c:
                first_norm(c)
                update(c + 1, 4 * c + 2)
                second_norm(c - 1)
                outer_moments(c, 4 * c + 4)
            first_norm(NC - 1)
            second_norm(NC - 2)
            outer_moments(NC - 1, 4 * NC - 2)
            second_norm(NC - 1)


def kernel(x, src, dst, edge_attr_32, L1_gnn_mW1, L1_gnn_mb1, L1_gnn_mW2, L1_gnn_mb2, L1_gnn_gW1, L1_gnn_gb1,
           L1_gnn_gW2, L1_gnn_gb2, L1_gnn_uW1, L1_gnn_ub1, L1_gnn_uW2, L1_gnn_ub2, L1_gnn_ln_g, L1_gnn_ln_b):
    import numpy as np
    import concourse.bacc as bacc
    from concourse.bass_utils import run_bass_kernel_spmd

    (x, src, dst, ea, mW1, mb1, mW2, mb2, gW1, gb1, gW2, gb2, uW1, ub1, uW2, ub2, ln_g, ln_b) = (
        np.asarray(a) for a in (
            x, src, dst, edge_attr_32, L1_gnn_mW1, L1_gnn_mb1, L1_gnn_mW2, L1_gnn_mb2, L1_gnn_gW1, L1_gnn_gb1,
            L1_gnn_gW2, L1_gnn_gb2, L1_gnn_uW1, L1_gnn_ub1, L1_gnn_uW2, L1_gnn_ub2, L1_gnn_ln_g, L1_gnn_ln_b))
    pad = NG * GE - E

    def rows_of(*parts):
        return np.concatenate([p.reshape(-1, p.shape[-1]) for p in parts], axis=0)

    src_l = np.concatenate([src, np.zeros(pad, src.dtype)]).reshape(NG, GT, P)
    dst_l = np.concatenate([dst, np.full(pad, N, dst.dtype)]).reshape(NG, GT, P)
    ea_l = np.concatenate([ea, np.zeros((pad, DE), ea.dtype)]).reshape(NG, 2, HALF, P, DE)
    node_w = np.concatenate([rows_of(gW1[:D], gb1), rows_of(mW1[:D], mb1)], axis=1)
    edge_w = np.concatenate([gW1[D:], mW1[D:]], axis=1)
    edge_w_apart = np.zeros((HALF, DE, HALF, D2), edge_w.dtype)
    for t in range(HALF):
        edge_w_apart[t, :, t] = edge_w
    ins = {
        "x": np.concatenate([x, np.zeros((NP - N, D), x.dtype)]).reshape(P, NT * D),
        "src": src_l.transpose(0, 2, 1),
        "dst": dst_l.transpose(2, 0, 1).reshape(P, NG * GT),
        "ea": ea_l.transpose(0, 2, 4, 1, 3).reshape(NG, P, 2 * P),
        "w_node": node_w,
        "w_edge": edge_w_apart.reshape(P, HALF * D2),
        "w_msg2": rows_of(mW2, mb2),
        "w_gate2": np.tile(gW2.reshape(1, D), (P, 1)),
        "b_gate2": np.tile(gb2.reshape(1, 1), (P, 1)),
        "w_upd1x": uW1[:D],
        "w_upd1a": uW1[D:],
        "b_upd1": ub1.reshape(D, 1),
        "w_upd2": rows_of(uW2, ub2),
        "ln_gb": np.tile(np.concatenate([ln_g, ln_b]).reshape(1, 2 * D), (P, 1)),
    }
    nc = bacc.Bacc("TRN2", target_bir_lowering=False, num_devices=1)
    arrays, args = {}, []
    for name, a in ins.items():
        a = np.ascontiguousarray(a)
        arrays[f"in_{name}"] = a
        args.append(nc.dram_tensor(f"in_{name}", a.shape, mybir.dt.from_np(a.dtype), kind="ExternalInput").ap())
    args.append(nc.dram_tensor("out_nodes", (P, NT * D), F32, kind="ExternalOutput").ap())
    bass_gnn(nc, *args)
    r = run_bass_kernel_spmd(nc, [arrays], core_ids=[0])
    return r.results[0]["out_nodes"].reshape(NP, D)[:N]
```
